# Optimizing a Trainium2 kernel written in Bass

```python
import numpy as np
import jax
import jax.numpy as jnp

def _softmax(x, axis=-1):
    return jax.nn.softmax(x, axis=axis)

def _gelu(x):
    return jax.nn.gelu(x, approximate=True)

def _silu(x):
    return jax.nn.silu(x)

def _sigmoid(x):
    return jax.nn.sigmoid(x)

def _layernorm(x, axis=-1, eps=1e-05):
    m = jnp.mean(x, axis=axis, keepdims=True)
    v = jnp.var(x, axis=axis, keepdims=True)
    return (x - m) / jnp.sqrt(v + eps)

def _scatter_add(tgt, idx, src, axis=0):
    return tgt.at[idx].add(src)

def _segment_sum(src, seg, n):
    return jax.ops.segment_sum(src, seg, n)
kernel_name = 'mk_lm_tower_d1_tok_ids2048_r4_3f160b'

def setup_inputs(seed: int=0):
    np.random.seed(seed)
    _w = jnp.asarray

    def _rec_inputs():
        import jax
        import jax.numpy as jnp
        _rk = jax.random.key(seed)
        x = jax.random.randint(jax.random.fold_in(_rk, 1), (16, 512), 0, 31999, jnp.int32)
        return x
    x = _rec_inputs()

    def _L0_tok_setup():
        import jax, jax.numpy as jnp
        import numpy as np
        VOCAB = 8000
        D = 512
        RANK = 16
        ALPHA = 32
        SCALING = ALPHA / RANK
        BATCH, SEQ = (4, 1024)
        key = jax.random.key(seed)
        k1, k2, k3, k4 = jax.random.split(key, 4)
        x = jax.random.randint(k1, (BATCH, SEQ), 0, VOCAB, dtype=jnp.int64 if jax.config.jax_enable_x64 else jnp.int32)
        embed_weight = jax.random.normal(k2, (VOCAB, D), dtype=jnp.float32)
        lora_A = jax.random.normal(k3, (VOCAB, RANK), dtype=jnp.float32) * 0.01
        lora_B = jax.random.normal(k4, (RANK, D), dtype=jnp.float32)
        return {'x': x, 'embed_weight': embed_weight, 'lora_A': lora_A, 'lora_B': lora_B}
    _L0_tok_all = _L0_tok_setup()
    _L0_tok_in = {k: v for k, v in _L0_tok_all.items() if k in ('embed_weight', 'lora_A', 'lora_B')}
    del _L0_tok_all

    def _L0_attn_setup():
        import jax, jax.numpy as jnp
        import numpy as np
        ETA = 0.01
        ALPHA = 0.95
        THRESHOLD = 1.0
        B, S, IN, OUT = (4, 512, 512, 512)

        def _reference_tuple_inner(x, W, target_W, delta_W):
            y = jnp.einsum('bsi,oi->bso', x, W + delta_W)
            predicted = jnp.einsum('bsi,oi->bso', x, target_W)
            teach = y - predicted
            surprise = jnp.mean(jnp.linalg.norm(teach, axis=-1))
            denom = jnp.float32(B * S)
            delta = jnp.einsum('bso,bsi->oi', teach, x) / denom
            new_delta_W = jnp.where(surprise > THRESHOLD, ALPHA * delta_W + ETA * delta, delta_W)
            return (y, new_delta_W)
        key = jax.random.key(seed)
        k1, k2, k3, k4 = jax.random.split(key, 4)
        bound = 1.0 / np.sqrt(IN)
        x = jax.random.normal(k1, (B, S, IN), dtype=jnp.float32)
        W = jax.random.uniform(k2, (OUT, IN), jnp.float32, -bound, bound)
        target_W = jax.random.uniform(k3, (OUT, IN), jnp.float32, -bound, bound)
        delta_W = 0.01 * jax.random.normal(k4, (OUT, IN), dtype=jnp.float32)
        return {'x': x, 'W': W, 'target_W': target_W, 'delta_W': delta_W}
    _L0_attn_all = _L0_attn_setup()
    _L0_attn_in = {k: v for k, v in _L0_attn_all.items() if k in ('W', 'target_W', 'delta_W')}
    del _L0_attn_all

    def _L0_ffn_setup():
        import jax, jax.numpy as jnp
        import numpy as np
        BLOCK = 128
        MAXVAL = 448.0

        def _quant_dequant(x_flat):
            xb = x_flat.reshape(-1, BLOCK)
            s = jnp.max(jnp.abs(xb), axis=1, keepdims=True) / MAXVAL
            q = (xb / s).astype(jnp.float8_e4m3fn)
            return (q.astype(jnp.float32) * s).reshape(x_flat.shape)
        key = jax.random.key(seed)
        k1, k2 = jax.random.split(key)
        B, T, D, OUT = (4, 1024, 512, 512)
        x = jax.random.normal(k1, (B, T, D), dtype=jnp.float32)
        limit = float(np.sqrt(6.0 / (D + OUT)))
        weight = jax.random.uniform(k2, (OUT, D), minval=-limit, maxval=limit, dtype=jnp.float32)
        return {'x': x, 'weight': weight}
    _L0_ffn_all = _L0_ffn_setup()
    _L0_ffn_in = {k: v for k, v in _L0_ffn_all.items() if k in ('weight',)}
    del _L0_ffn_all
    return {'x': x, 'L0_tok_embed_weight': _L0_tok_in['embed_weight'], 'L0_tok_lora_A': _L0_tok_in['lora_A'], 'L0_tok_lora_B': _L0_tok_in['lora_B'], 'L0_attn_W': _L0_attn_in['W'], 'L0_attn_target_W': _L0_attn_in['target_W'], 'L0_attn_delta_W': _L0_attn_in['delta_W'], 'L0_ffn_weight': _L0_ffn_in['weight']}

def reference(x, L0_tok_embed_weight, L0_tok_lora_A, L0_tok_lora_B, L0_attn_W, L0_attn_target_W, L0_attn_delta_W, L0_ffn_weight):
    import jax
    import jax.numpy as jnp

    def _L0_tok_ref(x, embed_weight, lora_A, lora_B):
        import jax, jax.numpy as jnp
        import numpy as np
        VOCAB = 8000
        D = 512
        RANK = 16
        ALPHA = 32
        SCALING = ALPHA / RANK
        BATCH, SEQ = (4, 1024)
        base = embed_weight[x]
        lora = jnp.einsum('bsr,rd->bsd', lora_A[x], lora_B) * SCALING
        return base + lora

    def _L0_attn_ref(x, W, target_W, delta_W):
        import jax, jax.numpy as jnp
        import numpy as np
        ETA = 0.01
        ALPHA = 0.95
        THRESHOLD = 1.0
        B, S, IN, OUT = (4, 512, 512, 512)

        def _reference_tuple_inner(x, W, target_W, delta_W):
            y = jnp.einsum('bsi,oi->bso', x, W + delta_W)
            predicted = jnp.einsum('bsi,oi->bso', x, target_W)
            teach = y - predicted
            surprise = jnp.mean(jnp.linalg.norm(teach, axis=-1))
            denom = jnp.float32(B * S)
            delta = jnp.einsum('bso,bsi->oi', teach, x) / denom
            new_delta_W = jnp.where(surprise > THRESHOLD, ALPHA * delta_W + ETA * delta, delta_W)
            return (y, new_delta_W)
        return _reference_tuple_inner(x, W, target_W, delta_W)[0]

    def _L0_ffn_ref(x, weight):
        import jax, jax.numpy as jnp
        import numpy as np
        BLOCK = 128
        MAXVAL = 448.0

        def _quant_dequant(x_flat):
            xb = x_flat.reshape(-1, BLOCK)
            s = jnp.max(jnp.abs(xb), axis=1, keepdims=True) / MAXVAL
            q = (xb / s).astype(jnp.float8_e4m3fn)
            return (q.astype(jnp.float32) * s).reshape(x_flat.shape)
        B, T, D = x.shape
        x_deq = _quant_dequant(x.reshape(-1)).reshape(B * T, D)
        w_deq = _quant_dequant(weight.reshape(-1)).reshape(weight.shape)
        out = x_deq @ w_deq.T
        return out.reshape(B, T, -1)
    h = _L0_tok_ref(x, L0_tok_embed_weight, L0_tok_lora_A, L0_tok_lora_B)
    h = h + _L0_attn_ref(_layernorm(h, axis=-1), L0_attn_W, L0_attn_target_W, L0_attn_delta_W)
    h = h + _L0_ffn_ref(_layernorm(h, axis=-1), L0_ffn_weight)
    return h

_drawn_inputs = setup_inputs


def setup_inputs(seed=0):
    import zlib

    import numpy as np

    out = dict(_drawn_inputs(seed))
    spreads = {}
    factors = {}
    for name, (base, spread) in spreads.items():
        noise = np.random.default_rng([zlib.crc32(name.encode()), seed]).standard_normal(out[name].shape)
        drawn = base * np.exp(spread * noise) if base else spread * noise
        out[name] = jnp.asarray(drawn.astype(out[name].dtype))
    for name, factor in factors.items():
        out[name] = (out[name] * factor).astype(out[name].dtype)
    return out
```

```python
from contextlib import ExitStack

import concourse.bass as bass
from concourse import mybir

P = 128
ALU = mybir.AluOpType
ACT = mybir.ActivationFunctionType
AX = mybir.AxisListType
F32 = mybir.dt.float32
F32R = mybir.dt.float32r
BF16 = mybir.dt.bfloat16
I32 = mybir.dt.int32

LORA_SCALING = 2.0
EPS = 1e-5
FP8_MAX = 448.0
FP8_BITS = 4
FP8_SUBNORMAL_STEP = 2.0**-9
LIFT = 2.0 ** (24 - FP8_BITS)
RASTER_FLOOR = 1.5 * 2.0**23 * FP8_SUBNORMAL_STEP


def token_tower(
    nc: bass.Bass,
    x: bass.AP,
    embed: bass.AP,
    lora_a: bass.AP,
    lora_b: bass.AP,
    attn_w: bass.AP,
    attn_delta: bass.AP,
    ffn_w: bass.AP,
    out: bass.AP,
):
    V, D = embed.shape
    R = lora_a.shape[1]
    KC = D // P
    x_flat = x.rearrange("b s -> (b s)")
    TILES = x_flat.shape[0] // P
    PAIRS = TILES // 2
    assert 8 * R == P

    x_dram = x_flat.rearrange("(p i) -> p i", i=TILES)
    out_dram = out.rearrange("b s d -> (b s) d").rearrange("(p i) d -> p i d", i=TILES)

    with ExitStack() as ctx:
        def sb(name, shape, dt=F32):
            return ctx.enter_context(nc.sbuf_tensor(name, shape, dt))

        def psum(name):
            return ctx.enter_context(nc.psum_tensor(name, [P, D], F32))

        def sem(name):
            return ctx.enter_context(nc.semaphore(name))

        ident = sb("ident", [P, P])
        neg_ident_r = sb("neg_ident_r", [P, P], F32R)
        ident_b = sb("ident_b", [P, P], BF16)
        neg_ident_b = sb("neg_ident_b", [P, P], BF16)
        minus_half = sb("minus_half", [P, 1])
        ones = sb("ones", [P, 2 * 2 * R])
        ids_raw = sb("ids_raw", [P, TILES], I32)
        ids_wrap = sb("ids_wrap", [P, TILES])
        ids_sum = sb("ids_sum", [P, TILES])
        ids = sb("ids", [P, TILES], I32)
        lora_b8 = sb("lora_b8", [P, D])
        lora_bh = sb("lora_bh", [P, D], F32R)
        lora_bs = sb("lora_bs", [P, D], F32R)
        wa_in = sb("wa_in", [P, KC, D])
        wd_in = sb("wd_in", [P, KC, D])
        wa_sum = sb("wa_sum", [P, KC])
        wf_in = sb("wf_in", [P, KC, D])
        wf_max = sb("wf_max", [P, KC * KC])
        wf_scale = sb("wf_scale", [P, KC * KC])
        wf_inv = sb("wf_inv", [P, KC * KC])
        wf_v = sb("wf_v", [P, KC, D])
        wf_abs = sb("wf_abs", [P, KC, D], BF16)
        wf_raster = sb("wf_raster", [P, KC, D], BF16)
        wf_t = sb("wf_t", [P, KC, D])
        wf_q = sb("wf_q", [P, KC, D])
        wf_deq = sb("wf_deq", [P, KC, D])
        wa_hi = sb("wa_hi", [P, KC, D], F32R)
        wa_lo = sb("wa_lo", [P, KC, D], F32R)
        wf_hi = sb("wf_hi", [P, KC, D], F32R)
        wf_lo = sb("wf_lo", [P, KC, D], F32R)

        ids_base = sb("ids_base", [P, 2], I32)
        ids_lora = sb("ids_lora", [P, 2], I32)
        base = [sb(f"base{u}", [P, D]) for u in range(2)]
        a_rows = sb("a_rows", [P, 2, R])
        a_split = sb("a_split", [P, 2, 4, R], F32R)
        a_t = sb("a_t", [P, P], F32R)
        h0 = [sb(f"h0_{u}", [P, D]) for u in range(2)]
        sum0 = [sb(f"sum0_{u}", [P, 1]) for u in range(2)]
        ssq0 = [sb(f"ssq0_{u}", [P, 1]) for u in range(2)]
        var0 = [sb(f"var0_{u}", [P, 1]) for u in range(2)]
        rstd0 = [sb(f"rstd0_{u}", [P, 1]) for u in range(2)]
        hi_t = [sb(f"hi_t{u}", [P, KC, P], F32R) for u in range(2)]
        lo_t = [sb(f"lo_t{u}", [P, KC, P], F32R) for u in range(2)]
        h1 = [sb(f"h1_{u}", [P, D]) for u in range(2)]
        sum1 = [sb(f"sum1_{u}", [P, 1]) for u in range(2)]
        cen = sb("cen", [P, D])
        ssq1 = [sb(f"ssq1_{u}", [P, 1]) for u in range(2)]
        var1 = [sb(f"var1_{u}", [P, 1]) for u in range(2)]
        rstd1 = [sb(f"rstd1_{u}", [P, 1]) for u in range(2)]
        bmax = [sb(f"bmax{u}", [P, KC]) for u in range(2)]
        binv = sb("binv", [P, KC])
        v = sb("v", [P, D])
        v_abs = sb("v_abs", [P, D], BF16)
        raster = sb("raster", [P, D], BF16)
        bscale = [sb(f"bscale{u}", [P, KC]) for u in range(2)]
        q_t = sb("q_t", [P, KC, P], F32R)
        part0 = sb("part0", [P, D])
        acc0 = sb("acc0", [P, D])
        outb = [sb(f"outb{u}", [P, D]) for u in range(2)]
        junk = sb("junk", [P, D], BF16)
        junk1 = sb("junk1", [P, D], BF16)

        lora_ps = psum("lora_ps")
        ht_ps = psum("ht_ps")
        y_ps = psum("y_ps")
        qt_ps = psum("qt_ps")
        ffn_ps = [psum(f"ffn_ps{b}") for b in range(KC)]
        banks = [lora_ps, ht_ps, y_ps, qt_ps, *ffn_ps]

        ids_landed, attn_landed, ffn_landed, lorab_landed = map(
            sem, ("ids_landed", "attn_landed", "ffn_landed", "lorab_landed"))
        zeroed, neg_ready, consts_ready, ids_step, ids_ready = map(
            sem, ("zeroed", "neg_ready", "consts_ready", "ids_step", "ids_ready"))
        lorab_hi, lorab_ready = map(sem, ("lorab_hi", "lorab_ready"))
        wa_step, wa_centred, wf_step, wf_abs_ready, wf_deq_ready = map(
            sem, ("wa_step", "wa_centred", "wf_step", "wf_abs_ready", "wf_deq_ready"))
        w_turned, w_hi_ready, w_lo_ready = map(sem, ("w_turned", "w_hi_ready", "w_lo_ready"))
        base_landed = [sem(f"base_landed{u}") for u in range(2)]
        a_landed = sem("a_landed")
        ids_set, ids_lora_set = sem("ids_set"), sem("ids_lora_set")
        a_hi_ready, a_split_ready = sem("a_hi_ready"), sem("a_split_ready")
        at_turned, at_ready = sem("at_turned"), sem("at_ready")
        lora_ready, h0_ready, ssq0_ready, var0_ready, rstd0_ready = map(
            sem, ("lora_ready", "h0_ready", "ssq0_ready", "var0_ready", "rstd0_ready"))
        ht_ready, hi_ready, rest_ready, lo_ready, y_ready = map(
            sem, ("ht_ready", "hi_ready", "rest_ready", "lo_ready", "y_ready"))
        h1_ready, cen_ready, ssq1_ready, var1_ready, rstd1_ready = map(
            sem, ("h1_ready", "cen_ready", "ssq1_ready", "var1_ready", "rstd1_ready"))
        bmax_ready, binv_ready, v_ready, v_abs_ready, raster_ready, bscale_ready = map(
            sem, ("bmax_ready", "binv_ready", "v_ready", "v_abs_ready", "raster_ready", "bscale_ready"))
        qt_turned, qt_ready = sem("qt_turned"), sem("qt_ready")
        ffn_ready = [sem(f"ffn_ready{b}") for b in range(KC)]
        part0_ready, acc_ready = sem("part0_ready"), sem("acc_ready")
        added = [acc_ready] + [sem(f"added{b}") for b in range(1, KC)]
        out_ready = added[-1]
        stored = [sem(f"stored{u}") for u in range(2)]

        def tile(k, u, d=0):
            return k + (u + d) // 2, (u + d) % 2

        def exists(k, u):
            return not isinstance(k, int) or 0 <= 2 * k + u < TILES

        def wait(eng, s, value):
            if not isinstance(value, int) or value > 0:
                eng.wait_ge(s, value)

        FIRST, LAST = -4, TILES
        LOOP = (1, PAIRS - 2)

        def steps(eng, step, before=None):
            for i in range(FIRST, 2 * LOOP[0]):
                if before:
                    before(i)
                step(i // 2, i % 2)
            with eng.Fori(*LOOP) as k:
                step(k, 0)
                step(k, 1)
            for i in range(2 * LOOP[1], LAST + 1):
                step(i // 2, i % 2)

        block = ctx.enter_context(nc.Block())

        @block.sync
        def _(sp):
            sp.dma_start(ids_raw[:], x_dram).then_inc(ids_landed, 16)
            for g in range(P // R):
                sp.dma_start(lora_b8[g * R:(g + 1) * R, :], lora_b).then_inc(lorab_landed, 16)
            sp.dma_start(wa_in[:], attn_w.rearrange("(c p) k -> p c k", p=P)).then_inc(attn_landed, 16)
            sp.dma_start(wd_in[:], attn_delta.rearrange("(c p) k -> p c k", p=P)).then_inc(attn_landed, 16)
            sp.dma_start(wf_in[:], ffn_w.rearrange("(c p) k -> p c k", p=P)).then_inc(ffn_landed, 16)

            def step(k, u):
                k, u = tile(k, u, -1)
                if exists(k, u):
                    wait(sp, out_ready, 2 * k + u + 1)
                    sp.dma_start(out_dram[:, bass.ds(2 * k + u, 1), :], outb[u][:].unsqueeze(1))\
                      .then_inc(stored[u], 16)

            steps(sp, step)
            for u in range(2):
                sp.wait_ge(stored[u], 16 * PAIRS)

        @block.gpsimd
        def _(pool):
            n = 0
            for t, fill in ((ident, 1.0), (ident_b, 1.0), (neg_ident_b, -1.0)):
                n += 1
                pool.memset(t[:], 0.0).then_inc(zeroed, 1)
                pool.wait_ge(zeroed, n)
                if t is ident:
                    pool.affine_select(out=neg_ident_r[:], in_=ident[:], compare_op=ALU.not_equal, fill=-1.0, base=0,
                                       pattern=[[-1, P]], channel_multiplier=1).then_inc(neg_ready, 1)
                    pool.wait_ge(neg_ready, 1)
                pool.affine_select(out=t[:], in_=t[:], compare_op=ALU.not_equal, fill=fill, base=0,
                                   pattern=[[-1, P]], channel_multiplier=1).then_inc(consts_ready, 1)
            pool.memset(minus_half[:], -0.5).then_inc(consts_ready, 1)
            pool.memset(ones[:], 1.0).then_inc(consts_ready, 1)
            pool.wait_ge(consts_ready, 5)
            pool.wait_ge(ids_ready, 1)

            def step(k, u):
                kn, un = tile(k, u, 1)
                if exists(kn, un):
                    wait(pool, var0_ready, 2 * kn + un + 1)
                    wait(pool, h1_ready, 2 * kn + un - 1)
                    pool.tensor_tensor(rstd0[un][:], var0[un][:], minus_half[:], ALU.pow).then_inc(rstd0_ready, 1)
                kg, ug = tile(k, u, 3)
                if exists(kg, ug):
                    pool.tensor_copy(ids_base[:, ug:ug + 1], ids[:, bass.ds(2 * kg + ug, 1)]).then_inc(ids_set, 1)
                lora_pair = u == 0 and exists(k + 2, 0)
                if lora_pair:
                    pool.tensor_copy(ids_lora[:], ids[:, bass.ds(2 * k + 4, 2)]).then_inc(ids_lora_set, 1)
                kp, up = tile(k, u, -1)
                if exists(kg, ug):
                    wait(pool, ids_set, 2 * kg + ug + 1)
                if lora_pair:
                    wait(pool, ids_lora_set, k + 3)
                if exists(kp, up):
                    wait(pool, bscale_ready, 2 * kp + up - 1)
                    wait(pool, var1_ready, 2 * kp + up + 1)
                    pool.tensor_tensor(rstd1[up][:], var1[up][:], minus_half[:], ALU.pow).then_inc(rstd1_ready, 1)
                if exists(kg, ug):
                    pool.indirect_dma_start(base[ug][:], None, embed,
                                            bass.IndirectOffsetOnAxis(ap=ids_base[:, ug:ug + 1], axis=0))\
                        .then_inc(base_landed[ug], 16)
                if lora_pair:
                    for t in range(2):
                        pool.indirect_dma_start(a_rows[:, t, :], None, lora_a,
                                                bass.IndirectOffsetOnAxis(ap=ids_lora[:, t:t + 1], axis=0))\
                            .then_inc(a_landed, 16)
                if exists(kp, up):
                    wait(pool, part0_ready, 2 * kp + up + 1)
                    wait(pool, added[1], 2 * kp + up)
                    pool.tensor_tensor(acc0[:], h1[up][:], part0[:], ALU.add).then_inc(added[0], 1)
                q = k + 2
                if u == 1 and exists(q, 0):
                    wait(pool, a_landed, 32 * q + 32)
                    wait(pool, at_turned, q)
                    rows = a_rows[:].unsqueeze(2)
                    pool.tensor_tensor(a_split[:, :, 0:1, :], rows, ones4.unsqueeze(2), ALU.mult).then_inc(a_hi_ready, 1)
                    wait(pool, a_hi_ready, q + 1)
                    pool.tensor_tensor(a_split[:, :, 1:2, :], rows, a_split[:, :, 0:1, :].bitcast(F32),
                                       ALU.subtract)
                    pool.tensor_tensor(a_split[:, :, 3:4, :], rows, a_split[:, :, 0:1, :].bitcast(F32),
                                       ALU.subtract)
                    pool.tensor_tensor(a_split[:, :, 2:3, :], rows, ones4.unsqueeze(2), ALU.mult)\
                        .then_inc(a_split_ready, 1)

            ones4 = ones[:, 0:2 * R].rearrange("p (t r) -> p t r", t=2)
            steps(pool, step)

        @block.scalar
        def _(act):
            def hi_of_weight(n, hi, c):
                act.wait_ge(w_turned, n + 1)
                act.activation(hi[:, c, :], banks[n][:], ACT.Copy, scale=1.0 / D if n < KC else 1.0)\
                   .then_inc(w_hi_ready, 1)

            for c in range(KC):
                hi_of_weight(c, wa_hi, c)

            def step(k, u):
                kn, un = tile(k, u, 1)
                kp, up = tile(k, u, -1)
                if exists(kn, un):
                    t = 2 * kn + un
                    wait(act, y_ready, t - 1)
                    wait(act, ht_ready, t + 1)
                    act.activation(hi_t[un][:].rearrange("p c t -> p (c t)"), ht_ps[:], ACT.Copy)\
                       .then_inc(hi_ready, 1)
                if exists(kp, up):
                    t = 2 * kp + up
                    wait(act, raster_ready, t)
                    wait(act, v_ready, t + 1)
                    act.activation(v_abs[:], v[:], ACT.Abs, scale=LIFT).then_inc(v_abs_ready, 1)
                    wait(act, var1_ready, t - 1)
                    wait(act, cen_ready, t + 1)
                    act.activation(junk1[:], cen[:], ACT.Square, accum_out=ssq1[up][:]).then_inc(ssq1_ready, 1)
                if u == 0 and exists(k + 1, 0):
                    wait(act, lora_ready, 2 * (k + 1))
                    wait(act, at_turned, k + 2)
                    act.activation(a_t[:], lora_ps[:, 0:P], ACT.Copy).then_inc(at_ready, 1)
                if exists(kn, un):
                    t = 2 * kn + un
                    wait(act, var0_ready, t - 1)
                    wait(act, h0_ready, t + 1)
                    act.activation(junk[:], h0[un][:], ACT.Square, bias=sum0[un][:], scale=-float(D),
                                   accum_out=ssq0[un][:]).then_inc(ssq0_ready, 1)
                if exists(kp, up):
                    t = 2 * kp + up
                    wait(act, ffn_ready[KC - 1], t)
                    wait(act, qt_turned, t + 1)
                    act.activation(q_t[:].rearrange("p c t -> p (c t)"), qt_ps[:], ACT.Copy).then_inc(qt_ready, 1)
                if exists(kn, un):
                    t = 2 * kn + un
                    wait(act, rest_ready, t + 1)
                    act.activation(lo_t[un][:].rearrange("p c t -> p (c t)"), ht_ps[:], ACT.Copy)\
                       .then_inc(lo_ready, 1)
                if exists(kp, up):
                    t = 2 * kp + up
                    wait(act, added[0], t)
                    wait(act, bscale_ready, t + 1)
                    wait(act, ffn_ready[0], t + 1)
                    act.activation(part0[:], ffn_ps[0][:], ACT.Copy, scale=bscale[up][:, 0:1])\
                       .then_inc(part0_ready, 1)

            def before(i):
                if i == 0:
                    act.wait_ge(wf_step, 3)
                    act.activation(wf_abs[:], wf_v[:], ACT.Abs, scale=LIFT).then_inc(wf_abs_ready, 1)
                    for c in range(KC):
                        hi_of_weight(KC + c, wf_hi, c)

            steps(act, step, before)

        @block.tensor
        def _(pe):
            pe.wait_ge(consts_ready, 5)

            def turn_weight(ready, w, first):
                pe.wait_ge(ready, 1)
                for c in range(KC):
                    for o in range(KC):
                        last = pe.transpose(banks[first + c][:, o * P:(o + 1) * P], w[:, o, c * P:(c + 1) * P], ident[:])
                    last.then_inc(w_turned, 1)

            turn_weight(wa_centred, wa_in, 0)

            def step(k, u):
                kn, un = tile(k, u, 1)
                kp, up = tile(k, u, -1)
                kl, ul = tile(k, u, 2)
                if exists(kn, un):
                    t = 2 * kn + un
                    wait(pe, lo_ready, t)
                    wait(pe, h0_ready, t + 1)
                    for c in range(KC):
                        last = pe.matmul(ht_ps[:, c * P:(c + 1) * P], h0[un][:, c * P:(c + 1) * P], ident[:],
                                         is_transpose=True, start=(c == 0), stop=False, skip_group_check=True)
                    last.then_inc(ht_ready, 1)
                if u == 0 and exists(k + 1, 0):
                    wait(pe, h0_ready, 2 * (k + 1))
                    wait(pe, a_split_ready, k + 2)
                    pe.transpose(lora_ps[:, 0:P], a_split[:].bitcast(F32).rearrange("p t s r -> p (t s r)"), ident[:])\
                      .then_inc(at_turned, 1)
                if exists(k, u):
                    wait(pe, h1_ready, 2 * k + u)
                    wait(pe, hi_ready, 2 * k + u + 1)
                    for c in range(KC):
                        pe.matmul(y_ps[:], hi_t[u][:, c, :], wa_hi[:, c, :], start=(c == 0), stop=False)
                        pe.matmul(y_ps[:], hi_t[u][:, c, :], wa_lo[:, c, :], start=False, stop=False)
                if exists(kp, up):
                    t = 2 * kp + up
                    wait(pe, qt_ready, t)
                    wait(pe, v_ready, t + 1)
                    wait(pe, raster_ready, t + 1)
                    for c in range(KC):
                        cs = slice(c * P, (c + 1) * P)
                        pe.matmul(qt_ps[:, cs], raster[:, cs], neg_ident_b[:], start=True, stop=False)
                        pe.matmul(qt_ps[:, cs], v[:, cs], ident[:], is_transpose=True, start=False, stop=False)
                        last = pe.matmul(qt_ps[:, cs], raster[:, cs], ident_b[:], start=False, stop=True)
                    last.then_inc(qt_turned, 1)
                if exists(kn, un):
                    wait(pe, hi_ready, 2 * kn + un + 1)
                    pe.matmul(ht_ps[:], neg_ident_r[:], hi_t[un][:].rearrange("p c t -> p (c t)"),
                              start=False, stop=True, skip_group_check=True).then_inc(rest_ready, 1)
                if exists(k, u):
                    wait(pe, lo_ready, 2 * k + u + 1)
                    for c in range(KC):
                        last = pe.matmul(y_ps[:], lo_t[u][:, c, :], wa_hi[:, c, :], start=False, stop=(c == KC - 1))
                    last.then_inc(y_ready, 1)
                if exists(kl, ul):
                    wait(pe, h0_ready, 2 * kl + ul)
                    wait(pe, at_ready, kl + 1)
                    rows = slice(ul * 4 * R, (ul + 1) * 4 * R)
                    pe.matmul(lora_ps[:], a_t[rows, :], lora_bs[rows, :], start=True, stop=True)\
                      .then_inc(lora_ready, 1)
                if exists(kp, up):
                    t = 2 * kp + up
                    for b in range(KC):
                        if b == 0:
                            wait(pe, part0_ready, t)
                            wait(pe, qt_ready, t + 1)
                        else:
                            wait(pe, added[b], t)
                        pe.matmul(ffn_ps[b][:], q_t[:, b, :], wf_hi[:, b, :], start=True, stop=False)
                        pe.matmul(ffn_ps[b][:], q_t[:, b, :], wf_lo[:, b, :], start=False, stop=True)\
                          .then_inc(ffn_ready[b], 1)

            def before(i):
                if i == FIRST:
                    pe.wait_ge(w_lo_ready, KC)
                    pe.wait_ge(lorab_ready, 1)
                if i == 0:
                    turn_weight(wf_deq_ready, wf_deq, KC)
                if i == 1:
                    pe.wait_ge(w_lo_ready, 2 * KC)

            steps(pe, step, before)

        @block.vector
        def _(dve):
            dve.wait_ge(ids_landed, 16)
            dve.tensor_scalar(ids_wrap[:], ids_raw[:], 0.0, float(V), ALU.is_lt, ALU.mult).then_inc(ids_step, 1)
            dve.wait_ge(ids_step, 1)
            dve.tensor_tensor(ids_sum[:], ids_raw[:], ids_wrap[:], ALU.add).then_inc(ids_step, 1)
            dve.wait_ge(ids_step, 2)
            dve.tensor_scalar(ids[:], ids_sum[:], float(V - 1), 0.0, ALU.min, ALU.max).then_inc(ids_ready, 1)

            dve.wait_ge(lorab_landed, 16 * (P // R))
            dve.tensor_scalar(lora_bh[:], lora_b8[:], LORA_SCALING, None, ALU.mult).then_inc(lorab_hi, 1)
            dve.wait_ge(lorab_hi, 1)
            for g in range(4):
                rows = slice(32 * g, 32 * (g + 1))
                if g % 2 == 0:
                    last = dve.tensor_copy(lora_bs[rows, :], lora_bh[rows, :].bitcast(F32))
                else:
                    last = dve.scalar_tensor_tensor(out=lora_bs[rows, :], in0=lora_b8[rows, :], scalar=LORA_SCALING,
                                                    in1=lora_bh[rows, :].bitcast(F32), op0=ALU.mult,
                                                    op1=ALU.subtract)
            last.then_inc(lorab_ready, 1)

            dve.wait_ge(attn_landed, 32)
            dve.tensor_tensor(wd_in[:], wa_in[:], wd_in[:], ALU.add).then_inc(wa_step, 1)
            dve.wait_ge(wa_step, 1)
            dve.tensor_reduce(wa_sum[:], wd_in[:], AX.X, ALU.add).then_inc(wa_step, 1)
            dve.wait_ge(wa_step, 2)
            for c in range(KC):
                last = dve.tensor_scalar(wa_in[:, c, :], wd_in[:, c, :], float(D), wa_sum[:, c:c + 1],
                                         ALU.mult, ALU.subtract)
            last.then_inc(wa_centred, 1)

            def lo_of_weight(n, hi, lo, c):
                dve.wait_ge(w_hi_ready, n + 1)
                dve.scalar_tensor_tensor(out=lo[:, c, :], in0=banks[n][:], scalar=1.0 / D if n < KC else 1.0,
                                         in1=hi[:, c, :].bitcast(F32), op0=ALU.mult, op1=ALU.subtract)\
                   .then_inc(w_lo_ready, 1)

            for c in range(KC):
                lo_of_weight(c, wa_hi, wa_lo, c)

            def blocks(t):
                return t.rearrange("p c (b k) -> p (c b) k", k=P)

            def ffn_weight():
                done = 0

                def then(ins):
                    nonlocal done
                    done += 1
                    ins.then_inc(wf_step, 1)
                    dve.wait_ge(wf_step, done)

                def spread(t):
                    return t[:].unsqueeze(2).to_broadcast([P, KC * KC, P])

                dve.wait_ge(ffn_landed, 16)
                then(dve.tensor_reduce(wf_max[:], blocks(wf_in[:]), AX.X, ALU.max, apply_absolute_value=True))
                dve.tensor_scalar(wf_scale[:], wf_max[:], 1.0 / FP8_MAX, None, ALU.mult)
                then(dve.reciprocal(wf_inv[:], wf_max[:]))
                then(dve.scalar_tensor_tensor(out=blocks(wf_v[:]), in0=blocks(wf_in[:]), scalar=FP8_MAX,
                                              in1=spread(wf_inv), op0=ALU.mult, op1=ALU.mult))
                dve.wait_ge(wf_abs_ready, 1)
                then(dve.tensor_scalar(wf_raster[:], wf_abs[:], RASTER_FLOOR, None, ALU.max))
                then(dve.tensor_tensor(wf_t[:], wf_raster[:], wf_v[:], ALU.subtract))
                then(dve.tensor_tensor(wf_q[:], wf_raster[:], wf_t[:], ALU.subtract))
                dve.tensor_tensor(blocks(wf_deq[:]), blocks(wf_q[:]), spread(wf_scale), ALU.mult)\
                   .then_inc(wf_deq_ready, 1)
                for c in range(KC):
                    lo_of_weight(KC + c, wf_hi, wf_lo, c)

            def before(i):
                if i == 0:
                    ffn_weight()

            def step(k, u):
                kn, un = tile(k, u, 1)
                kp, up = tile(k, u, -1)
                kl, ul = tile(k, u, 2)
                if exists(kp, up):
                    t = 2 * kp + up
                    wait(dve, rstd1_ready, t - 1)
                    wait(dve, ssq1_ready, t + 1)
                    dve.tensor_scalar(var1[up][:], ssq1[up][:], float(D) ** -3, EPS, ALU.mult, ALU.add)\
                       .then_inc(var1_ready, 1)
                if exists(kn, un):
                    t = 2 * kn + un
                    wait(dve, rstd0_ready, t - 1)
                    wait(dve, ssq0_ready, t + 1)
                    dve.tensor_scalar(var0[un][:], ssq0[un][:], float(D) ** -3, EPS, ALU.mult, ALU.add)\
                       .then_inc(var0_ready, 1)
                if exists(k, u):
                    t = 2 * k + u
                    wait(dve, added[0], t - 1)
                    wait(dve, cen_ready, t - 1)
                    wait(dve, rstd0_ready, t + 1)
                    wait(dve, y_ready, t + 1)
                    dve.scalar_tensor_tensor(out=h1[u][:], in0=y_ps[:], scalar=rstd0[u][:], in1=h0[u][:],
                                             op0=ALU.mult, op1=ALU.add, accum_out=sum1[u][:]).then_inc(h1_ready, 1)
                if exists(kl, ul):
                    t = 2 * kl + ul
                    wait(dve, ht_ready, t - 1)
                    wait(dve, h1_ready, t - 1)
                    wait(dve, base_landed[ul], 16 * (kl + 1))
                    wait(dve, lora_ready, t + 1)
                    dve.scalar_tensor_tensor(out=h0[ul][:], in0=lora_ps[:], scalar=1.0, in1=base[ul][:],
                                             op0=ALU.mult, op1=ALU.add, accum_out=sum0[ul][:]).then_inc(h0_ready, 1)
                if exists(kp, up):
                    t = 2 * kp + up
                    wait(dve, added[KC - 1], t - 1)
                    wait(dve, rstd1_ready, t + 1)
                    dve.tensor_scalar(bscale[up][:], bmax[up][:], rstd1[up][:], 1.0 / (FP8_MAX * D),
                                      ALU.mult, ALU.mult).then_inc(bscale_ready, 1)
                if exists(k, u):
                    t = 2 * k + u
                    wait(dve, ssq1_ready, t)
                    wait(dve, v_ready, t)
                    wait(dve, h1_ready, t + 1)
                    dve.tensor_scalar(cen[:], h1[u][:], float(D), sum1[u][:], ALU.mult, ALU.subtract)\
                       .then_inc(cen_ready, 1)
                    wait(dve, bscale_ready, t - 1)
                    wait(dve, cen_ready, t + 1)
                    dve.tensor_reduce(bmax[u][:], cen[:].rearrange("p (b k) -> p b k", k=P), AX.X, ALU.max,
                                      apply_absolute_value=True).then_inc(bmax_ready, 1)
                    wait(dve, bmax_ready, t + 1)
                    dve.reciprocal(binv[:], bmax[u][:]).then_inc(binv_ready, 1)
                    wait(dve, qt_turned, t)
                    wait(dve, v_abs_ready, t)
                    wait(dve, binv_ready, t + 1)
                    dve.scalar_tensor_tensor(out=v[:].rearrange("p (b k) -> p b k", k=P),
                                             in0=cen[:].rearrange("p (b k) -> p b k", k=P), scalar=FP8_MAX,
                                             in1=binv[:].unsqueeze(2).to_broadcast([P, KC, P]),
                                             op0=ALU.mult, op1=ALU.mult).then_inc(v_ready, 1)

                def add_block(b):
                    t = 2 * kp + up
                    if b == 1:
                        wait(dve, stored[up], 16 * kp)
                    wait(dve, added[b - 1], t + 1)
                    wait(dve, ffn_ready[b], t + 1)
                    dve.scalar_tensor_tensor(out=outb[up][:], in0=ffn_ps[b][:], scalar=bscale[up][:, b:b + 1],
                                             in1=acc0[:] if b == 1 else outb[up][:], op0=ALU.mult, op1=ALU.add)\
                       .then_inc(added[b], 1)

                if exists(kp, up):
                    add_block(1)
                if exists(k, u):
                    t = 2 * k + u
                    wait(dve, v_abs_ready, t + 1)
                    dve.tensor_scalar(raster[:], v_abs[:], RASTER_FLOOR, None, ALU.max).then_inc(raster_ready, 1)
                if exists(kp, up):
                    for b in range(2, KC):
                        add_block(b)

            steps(dve, step, before)


_INS = ["x", "L0_tok_embed_weight", "L0_tok_lora_A", "L0_tok_lora_B", "L0_attn_W", "L0_attn_delta_W", "L0_ffn_weight"]
_OUT = "out"


def kernel(**inputs):
    import numpy as _np
    import concourse.bacc as _bacc
    from concourse import mybir as _mybir
    from concourse.bass_utils import run_bass_kernel_spmd as _run

    nc = _bacc.Bacc("TRN2", target_bir_lowering=False, num_devices=1)
    arrays, args = {}, []
    for name in _INS:
        a = _np.ascontiguousarray(inputs[name])
        arrays[f"in_{name}_dram"] = a
        args.append(nc.dram_tensor(f"in_{name}_dram", a.shape, _mybir.dt.from_np(a.dtype), kind="ExternalInput").ap())
    shape = (*inputs["x"].shape, inputs["L0_tok_embed_weight"].shape[1])
    out = nc.dram_tensor(_OUT, shape, _mybir.dt.float32, kind="ExternalOutput").ap()
    token_tower(nc, *args, out)
    r = _run(nc, [arrays], core_ids=[0])
    return r.results[0][_OUT]
```

```python
from contextlib import ExitStack

import concourse.bass as bass
from concourse import mybir

P = 128
ALU = mybir.AluOpType
ACT = mybir.ActivationFunctionType
AX = mybir.AxisListType
F32 = mybir.dt.float32
F32R = mybir.dt.float32r
BF16 = mybir.dt.bfloat16
I32 = mybir.dt.int32

LORA_SCALING = 2.0
EPS = 1e-5
FP8_MAX = 448.0
FP8_BITS = 4
FP8_SUBNORMAL_STEP = 2.0**-9
LIFT = 2.0 ** (24 - FP8_BITS)
RASTER_FLOOR = 1.5 * 2.0**23 * FP8_SUBNORMAL_STEP


def token_tower(
    nc: bass.Bass,
    x: bass.AP,
    embed: bass.AP,
    lora_a: bass.AP,
    lora_b: bass.AP,
    attn_w: bass.AP,
    attn_delta: bass.AP,
    ffn_w: bass.AP,
    out: bass.AP,
):
    V, D = embed.shape
    R = lora_a.shape[1]
    KC = D // P
    x_flat = x.rearrange("b s -> (b s)")
    TILES = x_flat.shape[0] // P
    PAIRS = TILES // 2
    assert 8 * R == P

    x_dram = x_flat.rearrange("(p i) -> p i", i=TILES)
    out_dram = out.rearrange("b s d -> (b s) d").rearrange("(p i) d -> p i d", i=TILES)

    with ExitStack() as ctx:
        def sb(name, shape, dt=F32):
            return ctx.enter_context(nc.sbuf_tensor(name, shape, dt))

        def psum(name):
            return ctx.enter_context(nc.psum_tensor(name, [P, D], F32))

        def sem(name):
            return ctx.enter_context(nc.semaphore(name))

        ident = sb("ident", [P, P])
        neg_ident_r = sb("neg_ident_r", [P, P], F32R)
        ident_b = sb("ident_b", [P, P], BF16)
        neg_ident_b = sb("neg_ident_b", [P, P], BF16)
        minus_half = sb("minus_half", [P, 1])
        ones = sb("ones", [P, 2 * 2 * R])
        ids_raw = sb("ids_raw", [P, TILES], I32)
        ids_wrap = sb("ids_wrap", [P, TILES])
        ids_sum = sb("ids_sum", [P, TILES])
        ids = sb("ids", [P, TILES], I32)
        lora_b8 = sb("lora_b8", [P, D])
        lora_bh = sb("lora_bh", [P, D], F32R)
        lora_bs = sb("lora_bs", [P, D], F32R)
        wa_in = sb("wa_in", [P, KC, D])
        wd_in = sb("wd_in", [P, KC, D])
        wa_sum = sb("wa_sum", [P, KC])
        wf_in = sb("wf_in", [P, KC, D])
        wf_max = sb("wf_max", [P, KC * KC])
        wf_scale = sb("wf_scale", [P, KC * KC])
        wf_inv = sb("wf_inv", [P, KC * KC])
        wf_v = sb("wf_v", [P, KC, D])
        wf_abs = sb("wf_abs", [P, KC, D], BF16)
        wf_raster = sb("wf_raster", [P, KC, D], BF16)
        wf_t = sb("wf_t", [P, KC, D])
        wf_q = sb("wf_q", [P, KC, D])
        wf_deq = sb("wf_deq", [P, KC, D])
        wa_hi = sb("wa_hi", [P, KC, D], F32R)
        wa_lo = sb("wa_lo", [P, KC, D], F32R)
        wf_hi = sb("wf_hi", [P, KC, D], F32R)
        wf_lo = sb("wf_lo", [P, KC, D], F32R)

        ids_base = sb("ids_base", [P, 4], I32)
        ids_lora = sb("ids_lora", [P, 2], I32)
        base = [sb(f"base{u}", [P, D]) for u in range(4)]
        a_rows = sb("a_rows", [P, 2, R])
        a_split = sb("a_split", [P, 2, 4, R], F32R)
        a_t = sb("a_t", [P, P], F32R)
        h0 = [sb(f"h0_{u}", [P, D]) for u in range(4)]
        sum0 = [sb(f"sum0_{u}", [P, 1]) for u in range(2)]
        ssq0 = [sb(f"ssq0_{u}", [P, 1]) for u in range(2)]
        var0 = [sb(f"var0_{u}", [P, 1]) for u in range(2)]
        rstd0 = [sb(f"rstd0_{u}", [P, 1]) for u in range(2)]
        hi_t = [sb(f"hi_t{u}", [P, KC, P], F32R) for u in range(2)]
        lo_t = [sb(f"lo_t{u}", [P, KC, P], F32R) for u in range(2)]
        h1 = [sb(f"h1_{u}", [P, D]) for u in range(2)]
        sum1 = [sb(f"sum1_{u}", [P, 1]) for u in range(2)]
        cen = sb("cen", [P, D])
        ssq1 = [sb(f"ssq1_{u}", [P, 1]) for u in range(2)]
        var1 = [sb(f"var1_{u}", [P, 1]) for u in range(2)]
        rstd1 = [sb(f"rstd1_{u}", [P, 1]) for u in range(2)]
        bmax = [sb(f"bmax{u}", [P, KC]) for u in range(2)]
        binv = sb("binv", [P, KC])
        v = sb("v", [P, D])
        v_abs = sb("v_abs", [P, D], BF16)
        raster = sb("raster", [P, D], BF16)
        bscale = [sb(f"bscale{u}", [P, KC]) for u in range(2)]
        q_t = sb("q_t", [P, KC, P], F32R)
        part0 = [sb(f"part0_{u}", [P, D]) for u in range(2)]
        outb = [sb(f"outb{u}", [P, D]) for u in range(2)]
        junk = sb("junk", [P, D], BF16)
        junk1 = sb("junk1", [P, D], BF16)

        lora_ps = psum("lora_ps")
        ht_ps = psum("ht_ps")
        y_ps = psum("y_ps")
        qt_ps = psum("qt_ps")
        ffn_ps = [psum(f"ffn_ps{b}") for b in range(KC)]
        banks = [lora_ps, ht_ps, y_ps, qt_ps, *ffn_ps]

        ids_landed, attn_landed, ffn_landed, lorab_landed = map(
            sem, ("ids_landed", "attn_landed", "ffn_landed", "lorab_landed"))
        zeroed, neg_ready, consts_ready, ids_step, ids_ready = map(
            sem, ("zeroed", "neg_ready", "consts_ready", "ids_step", "ids_ready"))
        lorab_hi, lorab_ready = map(sem, ("lorab_hi", "lorab_ready"))
        wa_step, wa_centred, wf_step, wf_abs_ready, wf_deq_ready = map(
            sem, ("wa_step", "wa_centred", "wf_step", "wf_abs_ready", "wf_deq_ready"))
        w_turned, w_hi_ready, w_lo_ready = map(sem, ("w_turned", "w_hi_ready", "w_lo_ready"))
        base_landed = [sem(f"base_landed{u}") for u in range(4)]
        a_landed = sem("a_landed")
        ids_set, ids_lora_set = sem("ids_set"), sem("ids_lora_set")
        a_hi_ready, a_split_ready = sem("a_hi_ready"), sem("a_split_ready")
        at_turned, at_ready = sem("at_turned"), sem("at_ready")
        lora_ready, h0_ready, ssq0_ready, var0_ready, rstd0_ready = map(
            sem, ("lora_ready", "h0_ready", "ssq0_ready", "var0_ready", "rstd0_ready"))
        ht_ready, hi_ready, rest_ready, lo_ready, y_ready = map(
            sem, ("ht_ready", "hi_ready", "rest_ready", "lo_ready", "y_ready"))
        h1_ready, cen_ready, ssq1_ready, var1_ready, rstd1_ready = map(
            sem, ("h1_ready", "cen_ready", "ssq1_ready", "var1_ready", "rstd1_ready"))
        bmax_ready, binv_ready, v_ready, v_abs_ready, raster_ready, bscale_ready = map(
            sem, ("bmax_ready", "binv_ready", "v_ready", "v_abs_ready", "raster_ready", "bscale_ready"))
        qt_turned, qt_ready = sem("qt_turned"), sem("qt_ready")
        ffn_ready = [sem(f"ffn_ready{b}") for b in range(KC)]
        part0_ready, out_ready = sem("part0_ready"), sem("out_ready")
        added = [None] + [sem(f"added{b}") for b in range(1, KC)]
        stored = [sem(f"stored{u}") for u in range(2)]

        def tile(k, u, d=0):
            return k + (u + d) // 4, (u + d) % 4

        def pair(k, u):
            return 2 * k + u // 2

        def exists(k, u):
            return not isinstance(k, int) or 0 <= 4 * k + u < TILES

        def wait(eng, s, value):
            if not isinstance(value, int) or value > 0:
                eng.wait_ge(s, value)

        FIRST, LAST = -5, TILES + 1
        LOOP = (1, TILES // 4 - 2)

        def steps(eng, step, before=None):
            for i in range(FIRST, 4 * LOOP[0]):
                if before:
                    before(i)
                step(i // 4, i % 4)
            with eng.Fori(*LOOP) as k:
                for u in range(4):
                    step(k, u)
            for i in range(4 * LOOP[1], LAST + 1):
                step(i // 4, i % 4)

        block = ctx.enter_context(nc.Block())

        @block.sync
        def _(sp):
            sp.dma_start(ids_raw[:], x_dram).then_inc(ids_landed, 16)
            for g in range(P // R):
                sp.dma_start(lora_b8[g * R:(g + 1) * R, :], lora_b).then_inc(lorab_landed, 16)
            sp.dma_start(wa_in[:], attn_w.rearrange("(c p) k -> p c k", p=P)).then_inc(attn_landed, 16)
            sp.dma_start(wd_in[:], attn_delta.rearrange("(c p) k -> p c k", p=P)).then_inc(attn_landed, 16)
            sp.dma_start(wf_in[:], ffn_w.rearrange("(c p) k -> p c k", p=P)).then_inc(ffn_landed, 16)

            def step(k, u):
                k, u = tile(k, u, -2)
                if exists(k, u):
                    wait(sp, out_ready, 4 * k + u + 1)
                    sp.dma_start(out_dram[:, bass.ds(4 * k + u, 1), :], outb[u % 2][:].unsqueeze(1))\
                      .then_inc(stored[u % 2], 16)

            steps(sp, step)
            for u in range(2):
                sp.wait_ge(stored[u], 16 * PAIRS)

        @block.gpsimd
        def _(pool):
            n = 0
            for t, fill in ((ident, 1.0), (ident_b, 1.0), (neg_ident_b, -1.0)):
                n += 1
                pool.memset(t[:], 0.0).then_inc(zeroed, 1)
                pool.wait_ge(zeroed, n)
                if t is ident:
                    pool.affine_select(out=neg_ident_r[:], in_=ident[:], compare_op=ALU.not_equal, fill=-1.0, base=0,
                                       pattern=[[-1, P]], channel_multiplier=1).then_inc(neg_ready, 1)
                    pool.wait_ge(neg_ready, 1)
                pool.affine_select(out=t[:], in_=t[:], compare_op=ALU.not_equal, fill=fill, base=0,
                                   pattern=[[-1, P]], channel_multiplier=1).then_inc(consts_ready, 1)
            pool.memset(minus_half[:], -0.5).then_inc(consts_ready, 1)
            pool.memset(ones[:], 1.0).then_inc(consts_ready, 1)
            pool.wait_ge(consts_ready, 5)
            pool.wait_ge(ids_ready, 1)

            def step(k, u):
                kn, un = tile(k, u, 1)
                kp, up = tile(k, u, -1)
                kg, ug = tile(k, u, 4)
                kf, uf = tile(k, u, -2)
                ka, ua = tile(k, u, 5)
                gather_pair = u % 2 == 1 and exists(ka, ua)
                kc, uc = tile(k, u, 4)
                split_pair = u % 2 == 0 and exists(kc, uc)
                if exists(kn, un):
                    wait(pool, h1_ready, 4 * kn + un - 1)
                    wait(pool, var0_ready, 4 * kn + un + 1)
                    pool.tensor_tensor(rstd0[un % 2][:], var0[un % 2][:], minus_half[:], ALU.pow).then_inc(rstd0_ready, 1)
                if exists(kg, ug):
                    pool.tensor_copy(ids_base[:, ug:ug + 1], ids[:, bass.ds(4 * kg + ug, 1)]).then_inc(ids_set, 1)
                if gather_pair:
                    pool.tensor_copy(ids_lora[:], ids[:, bass.ds(4 * ka + ua, 2)]).then_inc(ids_lora_set, 1)
                if exists(kg, ug):
                    wait(pool, ids_set, 4 * kg + ug + 1)
                if gather_pair:
                    wait(pool, ids_lora_set, pair(ka, ua) + 1)
                if exists(kp, up):
                    wait(pool, bscale_ready, 4 * kp + up - 1)
                    wait(pool, var1_ready, 4 * kp + up + 1)
                    pool.tensor_tensor(rstd1[up % 2][:], var1[up % 2][:], minus_half[:], ALU.pow).then_inc(rstd1_ready, 1)
                if exists(kg, ug):
                    pool.indirect_dma_start(base[ug][:], None, embed,
                                            bass.IndirectOffsetOnAxis(ap=ids_base[:, ug:ug + 1], axis=0))\
                        .then_inc(base_landed[ug], 16)
                if gather_pair:
                    for t in range(2):
                        pool.indirect_dma_start(a_rows[:, t, :], None, lora_a,
                                                bass.IndirectOffsetOnAxis(ap=ids_lora[:, t:t + 1], axis=0))\
                            .then_inc(a_landed, 16)
                if exists(kf, uf):
                    t = 4 * kf + uf
                    wait(pool, part0_ready, t + 1)
                    wait(pool, added[KC - 1], t + 1)
                    pool.tensor_tensor(outb[uf % 2][:], outb[uf % 2][:], part0[uf % 2][:], ALU.add).then_inc(out_ready, 1)

                if split_pair:
                    q = pair(kc, uc)
                    wait(pool, a_landed, 32 * q + 32)
                    wait(pool, at_turned, q)
                    rows = a_rows[:].unsqueeze(2)
                    pool.tensor_tensor(a_split[:, :, 0:1, :], rows, ones4.unsqueeze(2), ALU.mult).then_inc(a_hi_ready, 1)
                    wait(pool, a_hi_ready, q + 1)
                    for c in (1, 3):
                        pool.tensor_tensor(a_split[:, :, c:c + 1, :], rows, a_split[:, :, 0:1, :].bitcast(F32),
                                           ALU.subtract)
                    pool.tensor_tensor(a_split[:, :, 2:3, :], rows, ones4.unsqueeze(2), ALU.mult)\
                        .then_inc(a_split_ready, 1)

            ones4 = ones[:, 0:2 * R].rearrange("p (t r) -> p t r", t=2)
            steps(pool, step)

        @block.scalar
        def _(act):
            def hi_of_weight(n, hi, c):
                act.wait_ge(w_turned, n + 1)
                act.activation(hi[:, c, :], banks[n][:], ACT.Copy, scale=1.0 / D if n < KC else 1.0)\
                   .then_inc(w_hi_ready, 1)

            for c in range(KC):
                hi_of_weight(c, wa_hi, c)

            def step(k, u):
                kn, un = tile(k, u, 1)
                kp, up = tile(k, u, -1)
                kl, ul = tile(k, u, 2)
                kq, uq = tile(k, u, 3)
                if u % 2 == 1 and exists(kq, uq):
                    wait(act, lora_ready, 4 * kq + uq)
                    wait(act, at_turned, pair(kq, uq) + 1)
                    act.activation(a_t[:], lora_ps[:, 0:P], ACT.Copy).then_inc(at_ready, 1)
                if exists(kp, up):
                    t = 4 * kp + up
                    wait(act, ffn_ready[KC - 1], t)
                    wait(act, qt_turned, t + 1)
                    act.activation(q_t[:].rearrange("p c t -> p (c t)"), qt_ps[:], ACT.Copy).then_inc(qt_ready, 1)
                if exists(k, u):
                    t = 4 * k + u
                    wait(act, v_ready, t)
                    wait(act, ssq1_ready, t)
                    wait(act, h1_ready, t + 1)
                    act.activation(cen[:], h1[u % 2][:], ACT.Identity, bias=sum1[u % 2][:], scale=-float(D))\
                       .then_inc(cen_ready, 1)
                if exists(kl, ul):
                    t = 4 * kl + ul
                    wait(act, y_ready, t - 1)
                    wait(act, ht_ready, t + 1)
                    act.activation(hi_t[ul % 2][:].rearrange("p c t -> p (c t)"), ht_ps[:], ACT.Copy)\
                       .then_inc(hi_ready, 1)
                if exists(kp, up):
                    t = 4 * kp + up
                    wait(act, out_ready, t - 1)
                    wait(act, bscale_ready, t + 1)
                    wait(act, ffn_ready[0], t + 1)
                    act.activation(part0[up % 2][:], ffn_ps[0][:], ACT.Copy, scale=bscale[up % 2][:, 0:1])\
                       .then_inc(part0_ready, 1)
                if exists(k, u):
                    t = 4 * k + u
                    wait(act, var1_ready, t - 1)
                    wait(act, cen_ready, t + 1)
                    act.activation(junk1[:], cen[:], ACT.Square, accum_out=ssq1[u % 2][:]).then_inc(ssq1_ready, 1)
                if exists(k, u):
                    t = 4 * k + u
                    wait(act, raster_ready, t)
                    wait(act, v_ready, t + 1)
                    act.activation(v_abs[:], v[:], ACT.Abs, scale=LIFT).then_inc(v_abs_ready, 1)
                if exists(kl, ul):
                    t = 4 * kl + ul
                    wait(act, var0_ready, t - 1)
                    wait(act, h0_ready, t + 1)
                    act.activation(junk[:], h0[ul][:], ACT.Square, bias=sum0[ul % 2][:], scale=-float(D),
                                   accum_out=ssq0[ul % 2][:]).then_inc(ssq0_ready, 1)
                if exists(kl, ul):
                    t = 4 * kl + ul
                    wait(act, y_ready, t - 1)
                    wait(act, rest_ready, t + 1)
                    act.activation(lo_t[ul % 2][:].rearrange("p c t -> p (c t)"), ht_ps[:], ACT.Copy)\
                       .then_inc(lo_ready, 1)

            def before(i):
                if i == 0:
                    act.wait_ge(wf_step, 3)
                    act.activation(wf_abs[:], wf_v[:], ACT.Abs, scale=LIFT).then_inc(wf_abs_ready, 1)
                    for c in range(KC):
                        hi_of_weight(KC + c, wf_hi, c)

            steps(act, step, before)

        @block.tensor
        def _(pe):
            pe.wait_ge(consts_ready, 5)

            def turn_weight(ready, w, first):
                pe.wait_ge(ready, 1)
                for c in range(KC):
                    for o in range(KC):
                        last = pe.transpose(banks[first + c][:, o * P:(o + 1) * P], w[:, o, c * P:(c + 1) * P], ident[:])
                    last.then_inc(w_turned, 1)

            turn_weight(wa_centred, wa_in, 0)

            def step(k, u):
                kn, un = tile(k, u, 1)
                kp, up = tile(k, u, -1)
                kl, ul = tile(k, u, 2)
                kq, uq = tile(k, u, 3)
                if exists(k, u):
                    wait(pe, h1_ready, 4 * k + u)
                    wait(pe, lo_ready, 4 * k + u + 1)
                    for c in range(KC):
                        pe.matmul(y_ps[:], hi_t[u % 2][:, c, :], wa_hi[:, c, :], start=(c == 0), stop=False)
                        pe.matmul(y_ps[:], hi_t[u % 2][:, c, :], wa_lo[:, c, :], start=False, stop=False)
                        last = pe.matmul(y_ps[:], lo_t[u % 2][:, c, :], wa_hi[:, c, :], start=False,
                                         stop=(c == KC - 1))
                    last.then_inc(y_ready, 1)
                if u % 2 == 1 and exists(kq, uq):
                    wait(pe, h0_ready, 4 * kq + uq)
                    wait(pe, a_split_ready, pair(kq, uq) + 1)
                    pe.transpose(lora_ps[:, 0:P], a_split[:].bitcast(F32).rearrange("p t s r -> p (t s r)"), ident[:])\
                      .then_inc(at_turned, 1)
                if exists(kp, up):
                    t = 4 * kp + up
                    wait(pe, qt_ready, t)
                    wait(pe, v_ready, t + 1)
                    wait(pe, raster_ready, t + 1)
                    for c in range(KC):
                        cs = slice(c * P, (c + 1) * P)
                        pe.matmul(qt_ps[:, cs], raster[:, cs], neg_ident_b[:], start=True, stop=False)
                        pe.matmul(qt_ps[:, cs], v[:, cs], ident[:], is_transpose=True, start=False, stop=False)
                        last = pe.matmul(qt_ps[:, cs], raster[:, cs], ident_b[:], start=False, stop=True)
                    last.then_inc(qt_turned, 1)
                if exists(kl, ul):
                    t = 4 * kl + ul
                    wait(pe, lo_ready, t)
                    wait(pe, h0_ready, t + 1)
                    for c in range(KC):
                        last = pe.matmul(ht_ps[:, c * P:(c + 1) * P], h0[ul][:, c * P:(c + 1) * P], ident[:],
                                         is_transpose=True, start=(c == 0), stop=False, skip_group_check=True)
                    last.then_inc(ht_ready, 1)
                if exists(kq, uq):
                    wait(pe, h0_ready, 4 * kq + uq)
                    wait(pe, at_ready, pair(kq, uq) + 1)
                    rows = slice(uq % 2 * 4 * R, (uq % 2 + 1) * 4 * R)
                    pe.matmul(lora_ps[:], a_t[rows, :], lora_bs[rows, :], start=True, stop=True)\
                      .then_inc(lora_ready, 1)
                if exists(kp, up):
                    t = 4 * kp + up
                    for b in range(KC):
                        if b == 0:
                            wait(pe, part0_ready, t)
                            wait(pe, qt_ready, t + 1)
                        else:
                            wait(pe, added[b], t)
                        pe.matmul(ffn_ps[b][:], q_t[:, b, :], wf_hi[:, b, :], start=True, stop=False)
                        pe.matmul(ffn_ps[b][:], q_t[:, b, :], wf_lo[:, b, :], start=False, stop=True)\
                          .then_inc(ffn_ready[b], 1)

                if exists(kl, ul):
                    wait(pe, hi_ready, 4 * kl + ul + 1)
                    pe.matmul(ht_ps[:], neg_ident_r[:], hi_t[ul % 2][:].rearrange("p c t -> p (c t)"),
                              start=False, stop=True, skip_group_check=True).then_inc(rest_ready, 1)

            def before(i):
                if i == FIRST:
                    pe.wait_ge(w_lo_ready, KC)
                    pe.wait_ge(lorab_ready, 1)
                if i == 0:
                    turn_weight(wf_deq_ready, wf_deq, KC)
                if i == 1:
                    pe.wait_ge(w_lo_ready, 2 * KC)

            steps(pe, step, before)

        @block.vector
        def _(dve):
            dve.wait_ge(ids_landed, 16)
            dve.tensor_scalar(ids_wrap[:], ids_raw[:], 0.0, float(V), ALU.is_lt, ALU.mult).then_inc(ids_step, 1)
            dve.wait_ge(ids_step, 1)
            dve.tensor_tensor(ids_sum[:], ids_raw[:], ids_wrap[:], ALU.add).then_inc(ids_step, 1)
            dve.wait_ge(ids_step, 2)
            dve.tensor_scalar(ids[:], ids_sum[:], float(V - 1), 0.0, ALU.min, ALU.max).then_inc(ids_ready, 1)

            dve.wait_ge(lorab_landed, 16 * (P // R))
            dve.tensor_scalar(lora_bh[:], lora_b8[:], LORA_SCALING, None, ALU.mult).then_inc(lorab_hi, 1)
            dve.wait_ge(lorab_hi, 1)
            for g in range(4):
                rows = slice(32 * g, 32 * (g + 1))
                if g % 2 == 0:
                    last = dve.tensor_copy(lora_bs[rows, :], lora_bh[rows, :].bitcast(F32))
                else:
                    last = dve.scalar_tensor_tensor(out=lora_bs[rows, :], in0=lora_b8[rows, :], scalar=LORA_SCALING,
                                                    in1=lora_bh[rows, :].bitcast(F32), op0=ALU.mult,
                                                    op1=ALU.subtract)
            last.then_inc(lorab_ready, 1)

            dve.wait_ge(attn_landed, 32)
            dve.tensor_tensor(wd_in[:], wa_in[:], wd_in[:], ALU.add).then_inc(wa_step, 1)
            dve.wait_ge(wa_step, 1)
            dve.tensor_reduce(wa_sum[:], wd_in[:], AX.X, ALU.add).then_inc(wa_step, 1)
            dve.wait_ge(wa_step, 2)
            for c in range(KC):
                last = dve.tensor_scalar(wa_in[:, c, :], wd_in[:, c, :], float(D), wa_sum[:, c:c + 1],
                                         ALU.mult, ALU.subtract)
            last.then_inc(wa_centred, 1)

            def lo_of_weight(n, hi, lo, c):
                dve.wait_ge(w_hi_ready, n + 1)
                dve.scalar_tensor_tensor(out=lo[:, c, :], in0=banks[n][:], scalar=1.0 / D if n < KC else 1.0,
                                         in1=hi[:, c, :].bitcast(F32), op0=ALU.mult, op1=ALU.subtract)\
                   .then_inc(w_lo_ready, 1)

            for c in range(KC):
                lo_of_weight(c, wa_hi, wa_lo, c)

            def blocks(t):
                return t.rearrange("p c (b k) -> p (c b) k", k=P)

            def ffn_weight():
                done = 0

                def then(ins):
                    nonlocal done
                    done += 1
                    ins.then_inc(wf_step, 1)
                    dve.wait_ge(wf_step, done)

                def spread(t):
                    return t[:].unsqueeze(2).to_broadcast([P, KC * KC, P])

                dve.wait_ge(ffn_landed, 16)
                then(dve.tensor_reduce(wf_max[:], blocks(wf_in[:]), AX.X, ALU.max, apply_absolute_value=True))
                dve.tensor_scalar(wf_scale[:], wf_max[:], 1.0 / FP8_MAX, None, ALU.mult)
                then(dve.reciprocal(wf_inv[:], wf_max[:]))
                then(dve.scalar_tensor_tensor(out=blocks(wf_v[:]), in0=blocks(wf_in[:]), scalar=FP8_MAX,
                                              in1=spread(wf_inv), op0=ALU.mult, op1=ALU.mult))
                dve.wait_ge(wf_abs_ready, 1)
                then(dve.tensor_scalar(wf_raster[:], wf_abs[:], RASTER_FLOOR, None, ALU.max))
                then(dve.tensor_tensor(wf_t[:], wf_raster[:], wf_v[:], ALU.subtract))
                then(dve.tensor_tensor(wf_q[:], wf_raster[:], wf_t[:], ALU.subtract))
                dve.tensor_tensor(blocks(wf_deq[:]), blocks(wf_q[:]), spread(wf_scale), ALU.mult)\
                   .then_inc(wf_deq_ready, 1)
                for c in range(KC):
                    lo_of_weight(KC + c, wf_hi, wf_lo, c)

            def before(i):
                if i == 0:
                    ffn_weight()

            def step(k, u):
                kn, un = tile(k, u, 1)
                kp, up = tile(k, u, -1)
                kl, ul = tile(k, u, 2)
                kf, uf = tile(k, u, -2)

                def add_block(kb, ub, b):
                    t = 4 * kb + ub
                    if b == 1:
                        wait(dve, bscale_ready, t + 1)
                        wait(dve, stored[ub % 2], 16 * pair(kb, ub))
                    else:
                        wait(dve, added[b - 1], t + 1)
                    wait(dve, ffn_ready[b], t + 1)
                    dve.scalar_tensor_tensor(out=outb[ub % 2][:], in0=ffn_ps[b][:], scalar=bscale[ub % 2][:, b:b + 1],
                                             in1=h1[ub % 2][:] if b == 1 else outb[ub % 2][:], op0=ALU.mult, op1=ALU.add)\
                       .then_inc(added[b], 1)

                if exists(kl, ul):
                    t = 4 * kl + ul
                    wait(dve, ht_ready, t - 3)
                    wait(dve, h1_ready, t - 3)
                    wait(dve, base_landed[ul], 16 * (kl + 1))
                    wait(dve, lora_ready, t + 1)
                    dve.scalar_tensor_tensor(out=h0[ul][:], in0=lora_ps[:], scalar=1.0, in1=base[ul][:],
                                             op0=ALU.mult, op1=ALU.add, accum_out=sum0[ul % 2][:]).then_inc(h0_ready, 1)
                if exists(k, u):
                    t = 4 * k + u
                    wait(dve, added[1], t - 1)
                    wait(dve, cen_ready, t - 1)
                    wait(dve, rstd0_ready, t + 1)
                    wait(dve, y_ready, t + 1)
                    dve.scalar_tensor_tensor(out=h1[u % 2][:], in0=y_ps[:], scalar=rstd0[u % 2][:], in1=h0[u][:],
                                             op0=ALU.mult, op1=ALU.add, accum_out=sum1[u % 2][:]).then_inc(h1_ready, 1)
                if exists(kp, up):
                    t = 4 * kp + up
                    wait(dve, rstd1_ready, t - 1)
                    wait(dve, ssq1_ready, t + 1)
                    dve.tensor_scalar(var1[up % 2][:], ssq1[up % 2][:], float(D) ** -3, EPS, ALU.mult, ALU.add)\
                       .then_inc(var1_ready, 1)
                if exists(kn, un):
                    t = 4 * kn + un
                    wait(dve, rstd0_ready, t - 1)
                    wait(dve, ssq0_ready, t + 1)
                    dve.tensor_scalar(var0[un % 2][:], ssq0[un % 2][:], float(D) ** -3, EPS, ALU.mult, ALU.add)\
                       .then_inc(var0_ready, 1)
                if exists(kf, uf):
                    for b in range(2, KC):
                        add_block(kf, uf, b)
                if exists(kp, up):
                    t = 4 * kp + up
                    wait(dve, added[KC - 1], t - 1)
                    wait(dve, part0_ready, t - 1)
                    wait(dve, rstd1_ready, t + 1)
                    dve.tensor_scalar(bscale[up % 2][:], bmax[up % 2][:], rstd1[up % 2][:], 1.0 / (FP8_MAX * D),
                                      ALU.mult, ALU.mult).then_inc(bscale_ready, 1)
                if exists(k, u):
                    t = 4 * k + u
                    wait(dve, bscale_ready, t - 1)
                    wait(dve, cen_ready, t + 1)
                    dve.tensor_reduce(bmax[u % 2][:], cen[:].rearrange("p (b k) -> p b k", k=P), AX.X, ALU.max,
                                      apply_absolute_value=True).then_inc(bmax_ready, 1)
                    wait(dve, bmax_ready, t + 1)
                    dve.reciprocal(binv[:], bmax[u % 2][:]).then_inc(binv_ready, 1)
                    wait(dve, qt_turned, t)
                    wait(dve, v_abs_ready, t)
                    wait(dve, binv_ready, t + 1)
                    dve.scalar_tensor_tensor(out=v[:].rearrange("p (b k) -> p b k", k=P),
                                             in0=cen[:].rearrange("p (b k) -> p b k", k=P), scalar=-FP8_MAX,
                                             in1=binv[:].unsqueeze(2).to_broadcast([P, KC, P]),
                                             op0=ALU.mult, op1=ALU.mult).then_inc(v_ready, 1)

                if exists(kp, up):
                    add_block(kp, up, 1)
                if exists(k, u):
                    t = 4 * k + u
                    wait(dve, v_abs_ready, t + 1)
                    dve.tensor_scalar(raster[:], v_abs[:], RASTER_FLOOR, None, ALU.max).then_inc(raster_ready, 1)

            steps(dve, step, before)


_INS = ["x", "L0_tok_embed_weight", "L0_tok_lora_A", "L0_tok_lora_B", "L0_attn_W", "L0_attn_delta_W", "L0_ffn_weight"]
_OUT = "out"


def kernel(**inputs):
    import numpy as _np
    import concourse.bacc as _bacc
    from concourse import mybir as _mybir
    from concourse.bass_utils import run_bass_kernel_spmd as _run

    nc = _bacc.Bacc("TRN2", target_bir_lowering=False, num_devices=1)
    arrays, args = {}, []
    for name in _INS:
        a = _np.ascontiguousarray(inputs[name])
        arrays[f"in_{name}_dram"] = a
        args.append(nc.dram_tensor(f"in_{name}_dram", a.shape, _mybir.dt.from_np(a.dtype), kind="ExternalInput").ap())
    shape = (*inputs["x"].shape, inputs["L0_tok_embed_weight"].shape[1])
    out = nc.dram_tensor(_OUT, shape, _mybir.dt.float32, kind="ExternalOutput").ap()
    token_tower(nc, *args, out)
    r = _run(nc, [arrays], core_ids=[0])
    return r.results[0][_OUT]
```

```python
from contextlib import ExitStack

import concourse.bass as bass
from concourse import mybir

P = 128
ALU = mybir.AluOpType
ACT = mybir.ActivationFunctionType
AX = mybir.AxisListType
F32 = mybir.dt.float32
F32R = mybir.dt.float32r
BF16 = mybir.dt.bfloat16
I32 = mybir.dt.int32

LORA_SCALING = 2.0
EPS = 1e-5
FP8_MAX = 448.0
FP8_BITS = 4
FP8_SUBNORMAL_STEP = 2.0**-9
LIFT = 2.0 ** (24 - FP8_BITS)
RASTER_FLOOR = 1.5 * 2.0**23 * FP8_SUBNORMAL_STEP


def token_tower(
    nc: bass.Bass,
    x: bass.AP,
    embed: bass.AP,
    lora_a: bass.AP,
    lora_b: bass.AP,
    attn_w: bass.AP,
    attn_delta: bass.AP,
    ffn_w: bass.AP,
    out: bass.AP,
):
    V, D = embed.shape
    R = lora_a.shape[1]
    KC = D // P
    x_flat = x.rearrange("b s -> (b s)")
    TILES = x_flat.shape[0] // P
    PAIRS = TILES // 2
    assert 8 * R == P

    x_dram = x_flat.rearrange("(p i) -> p i", i=TILES)
    out_dram = out.rearrange("b s d -> (b s) d").rearrange("(p i) d -> p i d", i=TILES)

    with ExitStack() as ctx:
        def sb(name, shape, dt=F32):
            return ctx.enter_context(nc.sbuf_tensor(name, shape, dt))

        def psum(name):
            return ctx.enter_context(nc.psum_tensor(name, [P, D], F32))

        def sem(name):
            return ctx.enter_context(nc.semaphore(name))

        ident = sb("ident", [P, P])
        neg_ident_r = sb("neg_ident_r", [P, P], F32R)
        ident_b = sb("ident_b", [P, P], BF16)
        neg_ident_b = sb("neg_ident_b", [P, P], BF16)
        minus_half = sb("minus_half", [P, 1])
        ones = sb("ones", [P, 2 * 2 * R])
        ids_raw = sb("ids_raw", [P, TILES], I32)
        ids_wrap = sb("ids_wrap", [P, TILES])
        ids_sum = sb("ids_sum", [P, TILES])
        ids = sb("ids", [P, TILES], I32)
        lora_b8 = sb("lora_b8", [P, D])
        lora_bh = sb("lora_bh", [P, D], F32R)
        lora_bs = sb("lora_bs", [P, D], F32R)
        wa_in = sb("wa_in", [P, KC, D])
        wd_in = sb("wd_in", [P, KC, D])
        wa_sum = sb("wa_sum", [P, KC])
        wf_in = sb("wf_in", [P, KC, D])
        wf_max = sb("wf_max", [P, KC * KC])
        wf_scale = sb("wf_scale", [P, KC * KC])
        wf_inv = sb("wf_inv", [P, KC * KC])
        wf_v = sb("wf_v", [P, KC, D])
        wf_abs = sb("wf_abs", [P, KC, D], BF16)
        wf_raster = sb("wf_raster", [P, KC, D], BF16)
        wf_t = sb("wf_t", [P, KC, D])
        wf_q = sb("wf_q", [P, KC, D])
        wf_deq = sb("wf_deq", [P, KC, D])
        wa_hi = sb("wa_hi", [P, KC, D], F32R)
        wa_lo = sb("wa_lo", [P, KC, D], F32R)
        wf_hi = sb("wf_hi", [P, KC, D], F32R)
        wf_lo = sb("wf_lo", [P, KC, D], F32R)

        ids_base = sb("ids_base", [P, 4], I32)
        ids_lora = sb("ids_lora", [P, 2], I32)
        base = [sb(f"base{u}", [P, D]) for u in range(4)]
        a_rows = sb("a_rows", [P, 2, R])
        a_split = sb("a_split", [P, 2, 4, R], F32R)
        a_t = sb("a_t", [P, P], F32R)
        h0 = [sb(f"h0_{u}", [P, D]) for u in range(4)]
        sum0 = [sb(f"sum0_{u}", [P, 1]) for u in range(2)]
        ssq0 = [sb(f"ssq0_{u}", [P, 1]) for u in range(2)]
        var0 = [sb(f"var0_{u}", [P, 1]) for u in range(2)]
        rstd0 = [sb(f"rstd0_{u}", [P, 1]) for u in range(2)]
        hi_t = [sb(f"hi_t{u}", [P, KC, P], F32R) for u in range(2)]
        lo_t = [sb(f"lo_t{u}", [P, KC, P], F32R) for u in range(2)]
        h1 = [sb(f"h1_{u}", [P, D]) for u in range(2)]
        sum1 = [sb(f"sum1_{u}", [P, 1]) for u in range(2)]
        cen = sb("cen", [P, D])
        ssq1 = [sb(f"ssq1_{u}", [P, 1]) for u in range(2)]
        var1 = [sb(f"var1_{u}", [P, 1]) for u in range(2)]
        rstd1 = [sb(f"rstd1_{u}", [P, 1]) for u in range(2)]
        bmax = [sb(f"bmax{u}", [P, KC]) for u in range(2)]
        binv = sb("binv", [P, KC])
        v = sb("v", [P, D])
        v_abs = sb("v_abs", [P, D], BF16)
        raster = sb("raster", [P, D], BF16)
        bscale = [sb(f"bscale{u}", [P, KC]) for u in range(2)]
        q_t = sb("q_t", [P, KC, P], F32R)
        part0 = [sb(f"part0_{u}", [P, D]) for u in range(2)]
        outb = [sb(f"outb{u}", [P, D]) for u in range(2)]
        junk = sb("junk", [P, D], BF16)
        junk1 = sb("junk1", [P, D], BF16)

        lora_ps = psum("lora_ps")
        ht_ps = psum("ht_ps")
        y_ps = psum("y_ps")
        qt_ps = psum("qt_ps")
        ffn_ps = [psum(f"ffn_ps{b}") for b in range(KC)]

        ids_landed, lorab_landed = sem("ids_landed"), sem("lorab_landed")
        attn_landed = [sem(f"attn_landed{o}") for o in range(KC)]
        ffn_landed = [sem(f"ffn_landed{o}") for o in range(KC)]
        zeroed, neg_ready, consts_ready, ids_step, ids_ready = map(
            sem, ("zeroed", "neg_ready", "consts_ready", "ids_step", "ids_ready"))
        lorab_hi, lorab_ready = map(sem, ("lorab_hi", "lorab_ready"))
        wa_summed, wa_centred = sem("wa_summed"), sem("wa_centred")
        wf_max_ready, wf_inv_ready, wf_v_ready, wf_abs_ready = map(
            sem, ("wf_max_ready", "wf_inv_ready", "wf_v_ready", "wf_abs_ready"))
        wf_rounding = [sem(f"wf_rounding{o}") for o in range(KC)]
        wf_deq_ready = [sem(f"wf_deq_ready{o}") for o in range(KC)]
        w_turned, w_hi_ready, w_lo_ready = map(sem, ("w_turned", "w_hi_ready", "w_lo_ready"))
        base_landed = [sem(f"base_landed{u}") for u in range(4)]
        a_landed = sem("a_landed")
        ids_set, ids_lora_set = sem("ids_set"), sem("ids_lora_set")
        a_hi_ready, a_split_ready = sem("a_hi_ready"), sem("a_split_ready")
        at_turned, at_ready = sem("at_turned"), sem("at_ready")
        lora_ready, h0_ready, ssq0_ready, var0_ready, rstd0_ready = map(
            sem, ("lora_ready", "h0_ready", "ssq0_ready", "var0_ready", "rstd0_ready"))
        ht_ready, hi_ready, rest_ready, lo_ready, y_ready = map(
            sem, ("ht_ready", "hi_ready", "rest_ready", "lo_ready", "y_ready"))
        h1_ready, cen_ready, ssq1_ready, var1_ready, rstd1_ready = map(
            sem, ("h1_ready", "cen_ready", "ssq1_ready", "var1_ready", "rstd1_ready"))
        bmax_ready, binv_ready, v_ready, v_abs_ready, raster_ready, bscale_ready = map(
            sem, ("bmax_ready", "binv_ready", "v_ready", "v_abs_ready", "raster_ready", "bscale_ready"))
        qt_turned, qt_ready = sem("qt_turned"), sem("qt_ready")
        ffn_ready = [sem(f"ffn_ready{b}") for b in range(KC)]
        part0_ready, out_ready = sem("part0_ready"), sem("out_ready")
        added = [None] + [sem(f"added{b}") for b in range(1, KC)]
        stored = [sem(f"stored{u}") for u in range(2)]

        def tile(k, u, d=0):
            return k + (u + d) // 4, (u + d) % 4

        def pair(k, u):
            return 2 * k + u // 2

        def exists(k, u):
            return not isinstance(k, int) or 0 <= 4 * k + u < TILES

        def wait(eng, s, value):
            if not isinstance(value, int) or value > 0:
                eng.wait_ge(s, value)

        FIRST, LAST = -5, TILES + 1
        LOOP = (1, TILES // 4 - 2)

        def steps(eng, step, before=None):
            for i in range(FIRST, 4 * LOOP[0]):
                if before:
                    before(i)
                step(i // 4, i % 4)
            with eng.Fori(*LOOP) as k:
                for u in range(4):
                    step(k, u)
            for i in range(4 * LOOP[1], LAST + 1):
                step(i // 4, i % 4)

        POOL_ROWS = 2

        def blocks(t):
            return t.rearrange("p (b k) -> p b k", k=P)

        def spread(t, o):
            return t[:, o * KC:(o + 1) * KC].unsqueeze(2).to_broadcast([P, KC, P])

        def round_weight(eng, chunks):
            for o in chunks:
                eng.wait_ge(wf_rounding[o], 1)
                eng.tensor_tensor(wf_t[:, o, :], wf_raster[:, o, :], wf_v[:, o, :], ALU.subtract)\
                   .then_inc(wf_rounding[o], 1)
            for o in chunks:
                eng.wait_ge(wf_rounding[o], 2)
                eng.tensor_tensor(wf_q[:, o, :], wf_raster[:, o, :], wf_t[:, o, :], ALU.subtract)\
                   .then_inc(wf_rounding[o], 1)
            for o in chunks:
                eng.wait_ge(wf_rounding[o], 3)
                eng.tensor_tensor(blocks(wf_deq[:, o, :]), blocks(wf_q[:, o, :]), spread(wf_scale, o), ALU.mult)\
                   .then_inc(wf_deq_ready[o], 1)

        block = ctx.enter_context(nc.Block())

        @block.sync
        def _(sp):
            sp.dma_start(ids_raw[:], x_dram).then_inc(ids_landed, 16)
            for o in range(KC):
                sp.dma_start(wf_in[:, o, :], ffn_w[o * P:(o + 1) * P, :]).then_inc(ffn_landed[o], 16)
            for o in range(KC):
                for dst, src in ((wa_in, attn_w), (wd_in, attn_delta)):
                    sp.dma_start(dst[:, o, :], src[o * P:(o + 1) * P, :]).then_inc(attn_landed[o], 16)

            def step(k, u):
                k, u = tile(k, u, -2)
                if exists(k, u):
                    wait(sp, out_ready, 4 * k + u + 1)
                    sp.dma_start(out_dram[:, bass.ds(4 * k + u, 1), :], outb[u % 2][:].unsqueeze(1))\
                      .then_inc(stored[u % 2], 16)

            steps(sp, step)
            for u in range(2):
                sp.wait_ge(stored[u], 16 * PAIRS)

        @block.gpsimd
        def _(pool):
            n = 0
            for t, fill in ((ident, 1.0), (ident_b, 1.0), (neg_ident_b, -1.0)):
                n += 1
                pool.memset(t[:], 0.0).then_inc(zeroed, 1)
                pool.wait_ge(zeroed, n)
                if t is ident:
                    pool.affine_select(out=neg_ident_r[:], in_=ident[:], compare_op=ALU.not_equal, fill=-1.0, base=0,
                                       pattern=[[-1, P]], channel_multiplier=1).then_inc(neg_ready, 1)
                    pool.wait_ge(neg_ready, 1)
                pool.affine_select(out=t[:], in_=t[:], compare_op=ALU.not_equal, fill=fill, base=0,
                                   pattern=[[-1, P]], channel_multiplier=1).then_inc(consts_ready, 1)
            pool.memset(minus_half[:], -0.5).then_inc(consts_ready, 1)
            pool.memset(ones[:], 1.0).then_inc(consts_ready, 1)
            pool.wait_ge(consts_ready, 5)
            pool.wait_ge(ids_ready, 1)

            def step(k, u):
                kn, un = tile(k, u, 1)
                kp, up = tile(k, u, -1)
                kg, ug = tile(k, u, 4)
                kf, uf = tile(k, u, -2)
                ka, ua = tile(k, u, 5)
                gather_pair = u % 2 == 1 and exists(ka, ua)
                kc, uc = tile(k, u, 4)
                split_pair = u % 2 == 0 and exists(kc, uc)
                if exists(kn, un):
                    wait(pool, h1_ready, 4 * kn + un - 1)
                    wait(pool, var0_ready, 4 * kn + un + 1)
                    pool.tensor_tensor(rstd0[un % 2][:], var0[un % 2][:], minus_half[:], ALU.pow)\
                        .then_inc(rstd0_ready, 1)
                if exists(kg, ug):
                    pool.tensor_copy(ids_base[:, ug:ug + 1], ids[:, bass.ds(4 * kg + ug, 1)]).then_inc(ids_set, 1)
                if gather_pair:
                    pool.tensor_copy(ids_lora[:], ids[:, bass.ds(4 * ka + ua, 2)]).then_inc(ids_lora_set, 1)
                if exists(kg, ug):
                    wait(pool, ids_set, 4 * kg + ug + 1)
                if gather_pair:
                    wait(pool, ids_lora_set, pair(ka, ua) + 1)
                if exists(kp, up):
                    wait(pool, bscale_ready, 4 * kp + up - 1)
                    wait(pool, var1_ready, 4 * kp + up + 1)
                    pool.tensor_tensor(rstd1[up % 2][:], var1[up % 2][:], minus_half[:], ALU.pow)\
                        .then_inc(rstd1_ready, 1)
                if exists(kg, ug):
                    pool.indirect_dma_start(base[ug][:], None, embed,
                                            bass.IndirectOffsetOnAxis(ap=ids_base[:, ug:ug + 1], axis=0))\
                        .then_inc(base_landed[ug], 16)
                if gather_pair:
                    for t in range(2):
                        pool.indirect_dma_start(a_rows[:, t, :], None, lora_a,
                                                bass.IndirectOffsetOnAxis(ap=ids_lora[:, t:t + 1], axis=0))\
                            .then_inc(a_landed, 16)
                if exists(kf, uf):
                    t = 4 * kf + uf
                    wait(pool, part0_ready, t + 1)
                    wait(pool, added[KC - 1], t + 1)
                    pool.tensor_tensor(outb[uf % 2][:], outb[uf % 2][:], part0[uf % 2][:], ALU.add)\
                        .then_inc(out_ready, 1)

                if split_pair:
                    q = pair(kc, uc)
                    wait(pool, a_landed, 32 * q + 32)
                    wait(pool, at_turned, q)
                    rows = a_rows[:].unsqueeze(2)
                    pool.tensor_tensor(a_split[:, :, 0:1, :], rows, ones4.unsqueeze(2), ALU.mult).then_inc(a_hi_ready, 1)
                    wait(pool, a_hi_ready, q + 1)
                    for c in (1, 3):
                        pool.tensor_tensor(a_split[:, :, c:c + 1, :], rows, a_split[:, :, 0:1, :].bitcast(F32),
                                           ALU.subtract)
                    pool.tensor_tensor(a_split[:, :, 2:3, :], rows, ones4.unsqueeze(2), ALU.mult)\
                        .then_inc(a_split_ready, 1)

            ones4 = ones[:, 0:2 * R].rearrange("p (t r) -> p t r", t=2)

            def before(i):
                if i == -2:
                    round_weight(pool, range(KC - POOL_ROWS, KC))

            steps(pool, step, before)

        @block.scalar
        def _(act):
            act.dma_start(lora_b8[:],
                          lora_b.unsqueeze(0).to_broadcast([P // R, R, D])).then_inc(lorab_landed, 16)
            act.wait_ge(lorab_landed, 16)
            act.activation(lora_bh[:], lora_b8[:], ACT.Copy, scale=LORA_SCALING).then_inc(lorab_hi, 1)
            for rows in (slice(0, 32), slice(64, 96)):
                act.activation(lora_bs[rows, :], lora_b8[rows, :], ACT.Copy, scale=LORA_SCALING)\
                   .then_inc(lorab_ready, 1)
            for o in range(KC):
                act.wait_ge(wf_v_ready, o + 1)
                act.activation(wf_abs[:, o, :], wf_v[:, o, :], ACT.Abs, scale=LIFT).then_inc(wf_abs_ready, 1)
            def turned_hi(done, hi, scale):
                for c in range(KC):
                    act.wait_ge(w_turned, done + c + 1)
                    act.activation(hi[:, c, :], ffn_ps[c][:], ACT.Copy, scale=scale).then_inc(w_hi_ready, 1)

            def step(k, u):
                kn, un = tile(k, u, 1)
                kp, up = tile(k, u, -1)
                kl, ul = tile(k, u, 2)
                kq, uq = tile(k, u, 3)
                if u % 2 == 1 and exists(kq, uq):
                    wait(act, lora_ready, 4 * kq + uq)
                    wait(act, at_turned, pair(kq, uq) + 1)
                    act.activation(a_t[:], lora_ps[:, 0:P], ACT.Copy).then_inc(at_ready, 1)
                if exists(kp, up):
                    t = 4 * kp + up
                    wait(act, ffn_ready[KC - 1], t)
                    wait(act, qt_turned, t + 1)
                    act.activation(q_t[:].rearrange("p c t -> p (c t)"), qt_ps[:], ACT.Copy).then_inc(qt_ready, 1)
                if exists(k, u):
                    t = 4 * k + u
                    wait(act, v_ready, t)
                    wait(act, ssq1_ready, t)
                    wait(act, h1_ready, t + 1)
                    act.activation(cen[:], h1[u % 2][:], ACT.Identity, bias=sum1[u % 2][:], scale=-float(D))\
                       .then_inc(cen_ready, 1)
                if exists(kl, ul):
                    t = 4 * kl + ul
                    wait(act, y_ready, t - 1)
                    wait(act, ht_ready, t + 1)
                    act.activation(hi_t[ul % 2][:].rearrange("p c t -> p (c t)"), ht_ps[:], ACT.Copy)\
                       .then_inc(hi_ready, 1)
                if exists(kp, up):
                    t = 4 * kp + up
                    wait(act, out_ready, t - 1)
                    wait(act, bscale_ready, t + 1)
                    wait(act, ffn_ready[0], t + 1)
                    act.activation(part0[up % 2][:], ffn_ps[0][:], ACT.Copy, scale=bscale[up % 2][:, 0:1])\
                       .then_inc(part0_ready, 1)
                if exists(k, u):
                    t = 4 * k + u
                    wait(act, var1_ready, t - 1)
                    wait(act, cen_ready, t + 1)
                    act.activation(junk1[:], cen[:], ACT.Square, accum_out=ssq1[u % 2][:]).then_inc(ssq1_ready, 1)
                if exists(k, u):
                    t = 4 * k + u
                    wait(act, raster_ready, t)
                    wait(act, v_ready, t + 1)
                    act.activation(v_abs[:], v[:], ACT.Abs, scale=LIFT).then_inc(v_abs_ready, 1)
                if exists(kl, ul):
                    t = 4 * kl + ul
                    wait(act, var0_ready, t - 1)
                    wait(act, h0_ready, t + 1)
                    act.activation(junk[:], h0[ul][:], ACT.Square, bias=sum0[ul % 2][:], scale=-float(D),
                                   accum_out=ssq0[ul % 2][:]).then_inc(ssq0_ready, 1)
                if exists(kl, ul):
                    t = 4 * kl + ul
                    wait(act, y_ready, t - 1)
                    wait(act, rest_ready, t + 1)
                    act.activation(lo_t[ul % 2][:].rearrange("p c t -> p (c t)"), ht_ps[:], ACT.Copy)\
                       .then_inc(lo_ready, 1)

            def before(i):
                if i == -1:
                    for o in range(KC):
                        act.wait_ge(wa_summed, o + 1)
                        act.activation(wa_in[:, o, :], wd_in[:, o, :], ACT.Identity, bias=wa_sum[:, o:o + 1],
                                       scale=-float(D)).then_inc(wa_centred, 1)
                    turned_hi(0, wa_hi, -1.0 / D)
                if i == 0:
                    turned_hi(KC, wf_hi, 1.0)

            steps(act, step, before)

        @block.tensor
        def _(pe):
            pe.wait_ge(consts_ready, 5)

            pe.wait_ge(lorab_ready, 4)

            def turn(w, o, c):
                return pe.transpose(ffn_ps[c][:, o * P:(o + 1) * P], w[:, o, c * P:(c + 1) * P], ident[:])

            def attention(u, first, end):
                for n in range(first, end):
                    c = n // 3
                    left = (hi_t, hi_t, lo_t)[n % 3][u % 2]
                    last = pe.matmul(y_ps[:], left[:, c, :], (wa_hi, wa_lo, wa_hi)[n % 3][:, c, :],
                                     start=(n == 0), stop=(n == 3 * KC - 1))
                return last

            def step(k, u):
                kn, un = tile(k, u, 1)
                kp, up = tile(k, u, -1)
                kl, ul = tile(k, u, 2)
                kq, uq = tile(k, u, 3)
                if exists(k, u):
                    wait(pe, lo_ready, 4 * k + u + 1)
                    attention(u, 2, 3 * KC).then_inc(y_ready, 1)
                if u % 2 == 1 and exists(kq, uq):
                    wait(pe, h0_ready, 4 * kq + uq)
                    wait(pe, a_split_ready, pair(kq, uq) + 1)
                    pe.transpose(lora_ps[:, 0:P], a_split[:].bitcast(F32).rearrange("p t s r -> p (t s r)"), ident[:])\
                      .then_inc(at_turned, 1)
                if exists(kp, up):
                    t = 4 * kp + up
                    wait(pe, qt_ready, t)
                    wait(pe, v_ready, t + 1)
                    wait(pe, raster_ready, t + 1)
                    for c in range(KC):
                        cs = slice(c * P, (c + 1) * P)
                        pe.matmul(qt_ps[:, cs], raster[:, cs], neg_ident_b[:], start=True, stop=False)
                        pe.matmul(qt_ps[:, cs], v[:, cs], ident[:], is_transpose=True, start=False, stop=False)
                        last = pe.matmul(qt_ps[:, cs], raster[:, cs], ident_b[:], start=False, stop=True)
                    last.then_inc(qt_turned, 1)
                if exists(kl, ul):
                    t = 4 * kl + ul
                    wait(pe, lo_ready, t)
                    wait(pe, h0_ready, t + 1)
                    for c in range(KC):
                        last = pe.matmul(ht_ps[:, c * P:(c + 1) * P], h0[ul][:, c * P:(c + 1) * P], ident[:],
                                         is_transpose=True, start=(c == 0), stop=False, skip_group_check=True)
                    last.then_inc(ht_ready, 1)
                if exists(kq, uq):
                    wait(pe, h0_ready, 4 * kq + uq)
                    wait(pe, at_ready, pair(kq, uq) + 1)
                    rows = slice(uq % 2 * 4 * R, (uq % 2 + 1) * 4 * R)
                    pe.matmul(lora_ps[:], a_t[rows, :], lora_bs[rows, :], start=True, stop=True)\
                      .then_inc(lora_ready, 1)
                if exists(kn, un):
                    if isinstance(kn, int) and (kn, un) == (0, 0):
                        pe.wait_ge(w_lo_ready, KC)
                    wait(pe, hi_ready, 4 * kn + un + 1)
                    wait(pe, h1_ready, 4 * kn + un)
                    attention(un, 0, 2)
                if exists(kp, up):
                    t = 4 * kp + up
                    if isinstance(kp, int) and t == 0:
                        pe.wait_ge(w_lo_ready, 2 * KC)
                    for b in range(KC):
                        if b == 0:
                            wait(pe, part0_ready, t)
                            wait(pe, qt_ready, t + 1)
                        else:
                            wait(pe, added[b], t)
                        pe.matmul(ffn_ps[b][:], q_t[:, b, :], wf_hi[:, b, :], start=True, stop=False)
                        pe.matmul(ffn_ps[b][:], q_t[:, b, :], wf_lo[:, b, :], start=False, stop=True)\
                          .then_inc(ffn_ready[b], 1)

                if exists(kl, ul):
                    wait(pe, hi_ready, 4 * kl + ul + 1)
                    pe.matmul(ht_ps[:], neg_ident_r[:], hi_t[ul % 2][:].rearrange("p c t -> p (c t)"),
                              start=False, stop=True, skip_group_check=True).then_inc(rest_ready, 1)

            def before(i):
                if i == -1:
                    for o in range(KC):
                        pe.wait_ge(wa_centred, o + 1)
                        for c in range(KC):
                            last = turn(wa_in, o, c)
                            if o == KC - 1:
                                last.then_inc(w_turned, 1)
                if i == 0:
                    for o in range(KC):
                        pe.wait_ge(wf_deq_ready[o], 1)
                    for c in range(KC):
                        pe.wait_ge(w_lo_ready, c + 1)
                        for o in range(KC):
                            last = turn(wf_deq, o, c)
                        last.then_inc(w_turned, 1)

            steps(pe, step, before)

        @block.vector
        def _(dve):
            dve.wait_ge(ids_landed, 16)
            dve.tensor_scalar(ids_wrap[:], ids_raw[:], 0.0, float(V), ALU.is_lt, ALU.mult).then_inc(ids_step, 1)
            dve.wait_ge(ids_step, 1)
            dve.tensor_tensor(ids_sum[:], ids_raw[:], ids_wrap[:], ALU.add).then_inc(ids_step, 1)
            dve.wait_ge(ids_step, 2)
            dve.tensor_scalar(ids[:], ids_sum[:], float(V - 1), 0.0, ALU.min, ALU.max).then_inc(ids_ready, 1)

            for o in range(KC):
                cols = slice(o * KC, (o + 1) * KC)
                dve.wait_ge(ffn_landed[o], 16)
                dve.tensor_reduce(wf_max[:, cols], blocks(wf_in[:, o, :]), AX.X, ALU.max,
                                  apply_absolute_value=True).then_inc(wf_max_ready, 1)
                dve.wait_ge(wf_max_ready, o + 1)
                dve.reciprocal(wf_inv[:, cols], wf_max[:, cols]).then_inc(wf_inv_ready, 1)
                dve.tensor_scalar(wf_scale[:, cols], wf_max[:, cols], 1.0 / FP8_MAX, None, ALU.mult)\
                   .then_inc(wf_inv_ready, 1)
                dve.wait_ge(wf_inv_ready, 2 * o + 2)
                dve.scalar_tensor_tensor(out=blocks(wf_v[:, o, :]), in0=blocks(wf_in[:, o, :]), scalar=FP8_MAX,
                                         in1=spread(wf_inv, o), op0=ALU.mult, op1=ALU.mult).then_inc(wf_v_ready, 1)
            dve.wait_ge(lorab_hi, 1)
            for rows in (slice(32, 64), slice(96, 128)):
                dve.scalar_tensor_tensor(out=lora_bs[rows, :], in0=lora_b8[rows, :], scalar=LORA_SCALING,
                                         in1=lora_bh[rows, :].bitcast(F32), op0=ALU.mult, op1=ALU.subtract)\
                   .then_inc(lorab_ready, 1)
            for o in reversed(range(KC)):
                dve.wait_ge(wf_abs_ready, KC)
                dve.tensor_scalar(wf_raster[:, o, :], wf_abs[:, o, :], RASTER_FLOOR, None, ALU.max)\
                   .then_inc(wf_rounding[o], 1)
            def step(k, u):
                kn, un = tile(k, u, 1)
                kp, up = tile(k, u, -1)
                kh, uh = tile(k, u, 3)
                kf, uf = tile(k, u, -2)

                def add_block(kb, ub, b):
                    t = 4 * kb + ub
                    if b == 1:
                        wait(dve, bscale_ready, t + 1)
                        wait(dve, stored[ub % 2], 16 * pair(kb, ub))
                    elif b > 2 or not exists(kb, ub + 2):
                        wait(dve, added[b - 1], t + 1)
                    wait(dve, ffn_ready[b], t + 1)
                    dve.scalar_tensor_tensor(out=outb[ub % 2][:], in0=ffn_ps[b][:], scalar=bscale[ub % 2][:, b:b + 1],
                                             in1=h1[ub % 2][:] if b == 1 else outb[ub % 2][:], op0=ALU.mult, op1=ALU.add)\
                       .then_inc(added[b], 1)

                if exists(k, u):
                    t = 4 * k + u
                    wait(dve, added[1], t - 1)
                    wait(dve, rstd0_ready, t + 1)
                    wait(dve, y_ready, t + 1)
                    dve.scalar_tensor_tensor(out=h1[u % 2][:], in0=y_ps[:], scalar=rstd0[u % 2][:], in1=h0[u][:],
                                             op0=ALU.mult, op1=ALU.add, accum_out=sum1[u % 2][:]).then_inc(h1_ready, 1)
                if exists(kp, up):
                    t = 4 * kp + up
                    wait(dve, ssq1_ready, t + 1)
                    dve.tensor_scalar(var1[up % 2][:], ssq1[up % 2][:], float(D) ** -3, EPS, ALU.mult, ALU.add)\
                       .then_inc(var1_ready, 1)
                if exists(kn, un):
                    t = 4 * kn + un
                    wait(dve, ssq0_ready, t + 1)
                    dve.tensor_scalar(var0[un % 2][:], ssq0[un % 2][:], float(D) ** -3, EPS, ALU.mult, ALU.add)\
                       .then_inc(var0_ready, 1)
                if exists(kf, uf):
                    for b in range(2, KC):
                        add_block(kf, uf, b)
                if exists(kp, up):
                    t = 4 * kp + up
                    wait(dve, rstd1_ready, t + 1)
                    dve.tensor_scalar(bscale[up % 2][:], bmax[up % 2][:], rstd1[up % 2][:], 1.0 / (FP8_MAX * D),
                                      ALU.mult, ALU.mult).then_inc(bscale_ready, 1)
                if exists(k, u):
                    t = 4 * k + u
                    wait(dve, cen_ready, t + 1)
                    dve.tensor_reduce(bmax[u % 2][:], cen[:].rearrange("p (b k) -> p b k", k=P), AX.X, ALU.max,
                                      apply_absolute_value=True).then_inc(bmax_ready, 1)
                    wait(dve, bmax_ready, t + 1)
                    dve.reciprocal(binv[:], bmax[u % 2][:]).then_inc(binv_ready, 1)
                    wait(dve, qt_turned, t)
                    wait(dve, binv_ready, t + 1)
                    dve.scalar_tensor_tensor(out=v[:].rearrange("p (b k) -> p b k", k=P),
                                             in0=cen[:].rearrange("p (b k) -> p b k", k=P), scalar=-FP8_MAX,
                                             in1=binv[:].unsqueeze(2).to_broadcast([P, KC, P]),
                                             op0=ALU.mult, op1=ALU.mult).then_inc(v_ready, 1)

                if exists(kh, uh):
                    t = 4 * kh + uh
                    wait(dve, base_landed[uh], 16 * (kh + 1))
                    wait(dve, lora_ready, t + 1)
                    dve.scalar_tensor_tensor(out=h0[uh][:], in0=lora_ps[:], scalar=1.0, in1=base[uh][:],
                                             op0=ALU.mult, op1=ALU.add, accum_out=sum0[uh % 2][:]).then_inc(h0_ready, 1)
                if exists(k, u):
                    t = 4 * k + u
                    wait(dve, v_abs_ready, t + 1)
                    dve.tensor_scalar(raster[:], v_abs[:], RASTER_FLOOR, None, ALU.max).then_inc(raster_ready, 1)
                if exists(kp, up):
                    add_block(kp, up, 1)

            def before(i):
                if i == -2:
                    dve.wait_ge(wf_v_ready, KC)
                    round_weight(dve, range(KC - POOL_ROWS))

                    for o in range(KC):
                        dve.wait_ge(attn_landed[o], 32)
                        dve.scalar_tensor_tensor(out=wd_in[:, o, :], in0=wa_in[:, o, :], scalar=1.0, in1=wd_in[:, o, :],
                                                 op0=ALU.mult, op1=ALU.add, accum_out=wa_sum[:, o:o + 1])\
                           .then_inc(wa_summed, 1)
                if i == -1:
                    for first, hi, lo, scale in ((0, wa_hi, wa_lo, -1.0 / D), (KC, wf_hi, wf_lo, 1.0)):
                        for c in range(KC):
                            dve.wait_ge(w_hi_ready, first + c + 1)
                            dve.scalar_tensor_tensor(out=lo[:, c, :], in0=ffn_ps[c][:], scalar=scale,
                                                     in1=hi[:, c, :].bitcast(F32), op0=ALU.mult, op1=ALU.subtract)\
                               .then_inc(w_lo_ready, 1)

            steps(dve, step, before)


_INS = ["x", "L0_tok_embed_weight", "L0_tok_lora_A", "L0_tok_lora_B", "L0_attn_W", "L0_attn_delta_W", "L0_ffn_weight"]
_OUT = "out"


def kernel(**inputs):
    import numpy as _np
    import concourse.bacc as _bacc
    from concourse import mybir as _mybir
    from concourse.bass_utils import run_bass_kernel_spmd as _run

    nc = _bacc.Bacc("TRN2", target_bir_lowering=False, num_devices=1)
    arrays, args = {}, []
    for name in _INS:
        a = _np.ascontiguousarray(inputs[name])
        arrays[f"in_{name}_dram"] = a
        args.append(nc.dram_tensor(f"in_{name}_dram", a.shape, _mybir.dt.from_np(a.dtype), kind="ExternalInput").ap())
    shape = (*inputs["x"].shape, inputs["L0_tok_embed_weight"].shape[1])
    out = nc.dram_tensor(_OUT, shape, _mybir.dt.float32, kind="ExternalOutput").ap()
    token_tower(nc, *args, out)
    r = _run(nc, [arrays], core_ids=[0])
    return r.results[0][_OUT]
```
